# Optimizing a Trainium2 kernel written in Bass

```python
import numpy as np
import jax
import jax.numpy as jnp

def _softmax(x, axis=-1):
    return jax.nn.softmax(x, axis=axis)

def _gelu(x):
    return jax.nn.gelu(x, approximate=True)

def _silu(x):
    return jax.nn.silu(x)

def _sigmoid(x):
    return jax.nn.sigmoid(x)

def _layernorm(x, axis=-1, eps=1e-05):
    m = jnp.mean(x, axis=axis, keepdims=True)
    v = jnp.var(x, axis=axis, keepdims=True)
    return (x - m) / jnp.sqrt(v + eps)

def _scatter_add(tgt, idx, src, axis=0):
    return tgt.at[idx].add(src)

def _segment_sum(src, seg, n):
    return jax.ops.segment_sum(src, seg, n)
kernel_name = 'mk_seq_preln_d1_jaxref_r4_a92396'

def setup_inputs(seed: int=0):
    np.random.seed(seed)
    _w = jnp.asarray

    def _L0_attn_setup():
        import jax, jax.numpy as jnp
        import numpy as np
        B, N, D = (4, 512, 256)
        H = 16
        HD = D // H
        SCALE = 1.0 / HD
        NEG = -10000.0
        THETA = 10000.0

        def _rope(t):
            d, n = (t.shape[-1], t.shape[-2])
            inv_freq = 1.0 / THETA ** (jnp.arange(0, d, 2, dtype=jnp.float32) / d)
            ang = jnp.arange(n, dtype=jnp.float32)[:, None] * inv_freq[None, :]
            cos = jnp.repeat(jnp.cos(ang), 2, axis=-1)
            sin = jnp.repeat(jnp.sin(ang), 2, axis=-1)
            x1, x2 = (t[..., ::2], t[..., 1::2])
            rot = jnp.stack([-x2, x1], axis=-1).reshape(t.shape)
            return t * cos + rot * sin
        key = jax.random.key(seed)
        ks = jax.random.split(key, 6)
        s = (1.0 / D) ** 0.5
        return {'x': jax.random.normal(ks[0], (B, N, D), jnp.float32), 'Wq': jax.random.normal(ks[1], (D, D), jnp.float32) * s, 'Wk': jax.random.normal(ks[2], (D, D), jnp.float32) * s, 'Wv': jax.random.normal(ks[3], (D, D), jnp.float32) * s, 'Wo': jax.random.normal(ks[4], (D, D), jnp.float32) * s, 'bo': jnp.zeros((D,), jnp.float32)}
    _L0_attn_in = _L0_attn_setup()

    def _L0_ffn_setup():
        import jax, jax.numpy as jnp
        import numpy as np
        D_MODEL = 256
        D_FF = 1024
        N_EXPERTS = 8
        D_EXPERT = D_FF // N_EXPERTS
        TOP_K = 2
        LB_WEIGHT = 0.01
        B, S = (4, 512)

        def _top_k_softmax(logits, k):
            vals, _ = jax.lax.top_k(logits, k)
            thresh = vals[..., -1:]
            masked = jnp.where(logits >= thresh, logits, -jnp.inf)
            return jax.nn.softmax(masked, axis=-1)
        key = jax.random.key(seed)
        ks = jax.random.split(key, 8)
        x = jax.random.normal(ks[0], (B, S, D_MODEL), dtype=jnp.float32)
        w1 = jax.random.normal(ks[1], (N_EXPERTS, D_MODEL, D_EXPERT), dtype=jnp.float32) * (1.0 / np.sqrt(D_MODEL))
        b1 = jnp.zeros((N_EXPERTS, D_EXPERT), dtype=jnp.float32)
        w2 = jax.random.normal(ks[2], (N_EXPERTS, D_EXPERT, D_MODEL), dtype=jnp.float32) * (1.0 / np.sqrt(D_EXPERT))
        b2 = jnp.zeros((N_EXPERTS, D_MODEL), dtype=jnp.float32)
        centroids = jax.random.normal(ks[3], (N_EXPERTS, D_MODEL), dtype=jnp.float32) * 0.02
        w_route = jax.random.normal(ks[4], (N_EXPERTS, D_MODEL), dtype=jnp.float32) * (1.0 / np.sqrt(D_MODEL))
        return {'x': x, 'w1': w1, 'b1': b1, 'w2': w2, 'b2': b2, 'centroids': centroids, 'w_route': w_route}
    _L0_ffn_in = _L0_ffn_setup()
    _d = {'L0_attn_x': _L0_attn_in['x'], 'L0_attn_Wq': _L0_attn_in['Wq'], 'L0_attn_Wk': _L0_attn_in['Wk'], 'L0_attn_Wv': _L0_attn_in['Wv'], 'L0_attn_Wo': _L0_attn_in['Wo'], 'L0_attn_bo': _L0_attn_in['bo'], 'L0_ffn_w1': _L0_ffn_in['w1'], 'L0_ffn_b1': _L0_ffn_in['b1'], 'L0_ffn_w2': _L0_ffn_in['w2'], 'L0_ffn_b2': _L0_ffn_in['b2'], 'L0_ffn_centroids': _L0_ffn_in['centroids'], 'L0_ffn_w_route': _L0_ffn_in['w_route']}
    _x0 = _d['L0_attn_x']
    _d['L0_attn_x'] = jax.random.normal(jax.random.fold_in(jax.random.key(seed), 1), (4, 2048, 256), dtype=_x0.dtype)
    del _x0
    return _d

def reference(L0_attn_x, L0_attn_Wq, L0_attn_Wk, L0_attn_Wv, L0_attn_Wo, L0_attn_bo, L0_ffn_w1, L0_ffn_b1, L0_ffn_w2, L0_ffn_b2, L0_ffn_centroids, L0_ffn_w_route):

    def _L0_attn_ref(x, Wq, Wk, Wv, Wo, bo):
        import jax, jax.numpy as jnp
        import numpy as np
        B, N, D = (4, 512, 256)
        H = 16
        HD = D // H
        SCALE = 1.0 / HD
        NEG = -10000.0
        THETA = 10000.0

        def _rope(t):
            d, n = (t.shape[-1], t.shape[-2])
            inv_freq = 1.0 / THETA ** (jnp.arange(0, d, 2, dtype=jnp.float32) / d)
            ang = jnp.arange(n, dtype=jnp.float32)[:, None] * inv_freq[None, :]
            cos = jnp.repeat(jnp.cos(ang), 2, axis=-1)
            sin = jnp.repeat(jnp.sin(ang), 2, axis=-1)
            x1, x2 = (t[..., ::2], t[..., 1::2])
            rot = jnp.stack([-x2, x1], axis=-1).reshape(t.shape)
            return t * cos + rot * sin
        b, n, _ = x.shape
        q = (x @ Wq.T).reshape(b, n, H, HD).transpose(0, 2, 1, 3)
        k = (x @ Wk.T).reshape(b, n, H, HD).transpose(0, 2, 1, 3)
        v = (x @ Wv.T).reshape(b, n, H, HD).transpose(0, 2, 1, 3)
        q = _rope(q)
        k = _rope(k)
        i = jnp.arange(n)
        add_mask = jnp.where(i[:, None] >= i[None, :], 0.0, NEG).astype(x.dtype)
        scores = jnp.einsum('bhqd,bhkd->bhqk', q, k) * SCALE + add_mask
        attn = jax.nn.softmax(scores, axis=-1)
        out = jnp.einsum('bhqk,bhkd->bhqd', attn, v)
        out = out.transpose(0, 2, 1, 3).reshape(b, n, H * HD)
        return out @ Wo.T + bo

    def _L0_ffn_ref(x, w1, b1, w2, b2, centroids, w_route):
        import jax, jax.numpy as jnp
        import numpy as np
        D_MODEL = 256
        D_FF = 1024
        N_EXPERTS = 8
        D_EXPERT = D_FF // N_EXPERTS
        TOP_K = 2
        LB_WEIGHT = 0.01
        B, S = (4, 512)

        def _top_k_softmax(logits, k):
            vals, _ = jax.lax.top_k(logits, k)
            thresh = vals[..., -1:]
            masked = jnp.where(logits >= thresh, logits, -jnp.inf)
            return jax.nn.softmax(masked, axis=-1)
        eps = 1e-12
        x_norm = x / jnp.maximum(jnp.linalg.norm(x, axis=-1, keepdims=True), eps)
        c_norm = centroids / jnp.maximum(jnp.linalg.norm(centroids, axis=-1, keepdims=True), eps)
        cos_scores = jnp.einsum('bsd,ed->bse', x_norm, c_norm)
        route_scores = jnp.einsum('bsd,ed->bse', x, w_route)
        logits = cos_scores + route_scores
        gates = _top_k_softmax(logits, TOP_K)
        h = jax.nn.gelu(jnp.einsum('bsd,edh->bseh', x, w1) + b1, approximate=False)
        expert_out = jnp.einsum('bseh,ehd->bsed', h, w2) + b2
        out = jnp.einsum('bse,bsed->bsd', gates, expert_out)
        return out
    x = L0_attn_x
    x = x + _L0_attn_ref(_layernorm(x, axis=-1), L0_attn_Wq, L0_attn_Wk, L0_attn_Wv, L0_attn_Wo, L0_attn_bo)
    x = x + _L0_ffn_ref(_layernorm(x, axis=-1), L0_ffn_w1, L0_ffn_b1, L0_ffn_w2, L0_ffn_b2, L0_ffn_centroids, L0_ffn_w_route)
    return x

_drawn_inputs = setup_inputs


def setup_inputs(seed=0):
    import zlib

    import numpy as np

    out = dict(_drawn_inputs(seed))
    spreads = {'L0_attn_bo': (0.0, 0.1), 'L0_ffn_b1': (0.0, 0.1), 'L0_ffn_b2': (0.0, 0.1)}
    factors = {}
    for name, (base, spread) in spreads.items():
        noise = np.random.default_rng([zlib.crc32(name.encode()), seed]).standard_normal(out[name].shape)
        drawn = base * np.exp(spread * noise) if base else spread * noise
        out[name] = jnp.asarray(drawn.astype(out[name].dtype))
    for name, factor in factors.items():
        out[name] = (out[name] * factor).astype(out[name].dtype)
    return out
```

```python
from contextlib import ExitStack

import concourse.bass as bass
from concourse import mybir

F32 = mybir.dt.float32
BF16 = mybir.dt.bfloat16
ALU = mybir.AluOpType
ACT = mybir.ActivationFunctionType
AX = mybir.AxisListType

P = 128
B, N, D = 4, 2048, 256
H, HD = 16, 16
E, F = 8, 128
CH = 512
NC = N // CH
NCH = B * NC
TT = CH // P
KD = D // P
JH = 4
NG = H // JH
NKB = N // P
R = 6
QPART = (0, 0, 1, 1, 0, 2)
KPART = (0, 1, 0, 1, 2, 0)
LEAD = 2


def done(n):
    return n + 1 + LEAD


def two_before(n):
    return n - 1 + LEAD


def wait_alone(eng, semaphore, value, passed):
    eng.wait_ge(semaphore, value)
    eng.sem_inc(passed, 1)


def layer_kernel(nc, x, wqk, wv, wo, bo, w1, b1, w2, b2, cent, wr, cos, sin, tri, ident, out):
    ctx = ExitStack()
    with ctx:
        def sb(name, shape, dt=F32):
            return ctx.enter_context(nc.sbuf_tensor(name, shape, dt))

        def sem(name):
            return ctx.enter_context(nc.semaphore(name))

        parts_dram = nc.dram_tensor("parts_dram", (3, 2, NCH, D, CH), BF16, kind="Internal").ap()
        v_dram = nc.dram_tensor("v_dram", (B, P, NG, NKB, JH * 2 * HD), F32, kind="Internal").ap()
        att_dram = nc.dram_tensor("att_dram", (NCH, D, CH), F32, kind="Internal").ap()

        bank = ctx.enter_context(nc.psum_tensor("bank", [P, 8, CH], F32))

        ident_sb = sb("ident_sb", [P, P])
        load_const(nc, ctx, sb, sem, ident, ident_sb)
        with ExitStack() as s1:
            project(nc, s1, x, wqk, wv, cos, sin, ident_sb, bank, parts_dram, v_dram)
        with ExitStack() as s2:
            attend(nc, s2, tri, bank, parts_dram, v_dram, att_dram)
        with ExitStack() as s3:
            experts(nc, s3, x, wo, bo, w1, b1, w2, b2, cent, wr, ident_sb, bank, att_dram, out)


def load_const(nc, ctx, sb, sem, ident, ident_sb):
    loaded = sem("ident_loaded")
    with nc.Block() as block:
        @block.sync
        def _(sp):
            sp.dma_start(ident_sb[:], ident).then_inc(loaded, 16)
            sp.wait_ge(loaded, 16)


def project(nc, ctx, x, wqk, wv, cos, sin, ident_sb, bank, parts_dram, v_dram):
    def sb(name, shape, dt=F32):
        return ctx.enter_context(nc.sbuf_tensor(name, shape, dt))

    def sem(name):
        return ctx.enter_context(nc.semaphore(name))

    NT = 2 * KD
    wqk_sb = sb("wqk_sb", [P, KD, 2 * D])
    wv_sb = sb("wv_sb", [P, KD, D])
    cos_sb = sb("cos_sb", [P, N])
    sin_sb = sb("sin_sb", [P, N])
    x_sb = [sb(f"a_x{u}", [P, TT, D]) for u in range(2)]
    xn = [sb(f"a_xn{u}", [P, TT, D]) for u in range(2)]
    xnT = [sb(f"a_xnT{u}", [P, KD, CH]) for u in range(2)]
    stats = sb("a_stats", [P, TT, 6])
    mv = sb("a_mv", [P, TT, 2])
    std = sb("a_std", [P, TT, 1])
    rstd = sb("a_rstd", [P, TT, 1])
    eps = sb("a_eps", [P, 1])
    cosed = [sb(f"a_cosed{k}", [P, CH]) for k in range(2)]
    swapped = [sb(f"a_swapped{k}", [P, CH]) for k in range(2)]
    rot = [sb(f"a_rot{u}", [P, NT, CH]) for u in range(2)]
    rest = [sb(f"a_rest{u}", [P, NT, CH]) for u in range(2)]
    parts = [sb(f"a_parts{u}", [P, 3, NT, CH], BF16) for u in range(2)]
    v_sb = [sb(f"a_v{u}", [P, TT, H, 2 * HD]) for u in range(2)]

    passed = sem("a_passed")
    weights_loaded = sem("a_weights_loaded")
    x_loaded = [sem(f"a_x_loaded{u}") for u in range(2)]
    parts_stored = [sem(f"a_parts_stored{u}") for u in range(2)]
    v_stored = [sem(f"a_v_stored{u}") for u in range(2)]
    consts_set = sem("a_consts_set")
    ln_step = sem("a_ln_step")
    var_ready = sem("a_var_ready")
    std_ready = sem("a_std_ready")
    xn_ready = sem("a_xn_ready")
    xnT_summed = sem("a_xnT_summed")
    xnT_ready = sem("a_xnT_ready")
    qk_summed = sem("a_qk_summed")
    v_summed = sem("a_v_summed")
    v_ready = sem("a_v_ready")
    rope_step = sem("a_rope_step")
    rot_ready = sem("a_rot_ready")
    part0_ready = sem("a_part0_ready")
    rest_ready = sem("a_rest_ready")
    part1_ready = sem("a_part1_ready")
    part2_ready = sem("a_part2_ready")

    LN_STEPS, ROPE_STEPS = 2, 3 * NT

    def over_chunks(body):
        def run(eng):
            with eng.Fori(0, B - 1) as b:
                for c in range(NC):
                    body(eng, b, c, False)
            for c in range(NC):
                body(eng, B - 1, c, c == NC - 1)
        return run

    def halves(b, c):
        return b * (NC // 2) + c // 2 + 1

    with nc.Block() as block:
        @block.sync
        def _(sp):
            def load_x(n, u):
                sp.dma_start(x_sb[u][:], x[bass.ds(n * CH, CH), :].rearrange("(t p) d -> p t d", p=P))\
                  .then_inc(x_loaded[u], 16)

            load_x(0, 0)
            sp.dma_start(wqk_sb[:], wqk.rearrange("(k p) n -> p k n", p=P)).then_inc(weights_loaded, 16)
            sp.dma_start(wv_sb[:], wv.rearrange("(k p) n -> p k n", p=P)).then_inc(weights_loaded, 16)
            sp.dma_start(cos_sb[:], cos).then_inc(weights_loaded, 16)
            sp.dma_start(sin_sb[:], sin).then_inc(weights_loaded, 16)
            load_x(1, 1)

            def body(sp, b, c, last):
                n, u = b * NC + c, c % 2
                if not (isinstance(n, int) and n + 2 >= NCH):
                    wait_alone(sp, xn_ready, done(n), passed)
                    load_x(n + 2, u)
                wait_alone(sp, v_ready, done(n), passed)
                for t in range(TT):
                    sp.dma_start(v_dram[bass.ds(b, 1), :, :, c * TT + t, :].rearrange("o p g r -> p (o g) r"),
                                 v_sb[u][:, t].rearrange("p (g j) r -> p g (j r)", g=NG)).then_inc(v_stored[u], 16)
                wait_alone(sp, part2_ready, done(n) * NT, passed)
                for i in range(3):
                    for q in range(2):
                        sp.dma_start(parts_dram[i, q, bass.ds(n, 1), :, :].rearrange("o (k p) t -> p (o k) t", p=P),
                                     parts[u][:, i, KD * q:KD * (q + 1)]).then_inc(parts_stored[u], 16)

            over_chunks(body)(sp)
            for u in range(2):
                sp.wait_ge(v_stored[u], 16 * TT * (NCH // 2 + 1))
                sp.wait_ge(parts_stored[u], 16 * 6 * (NCH // 2 + 1))

        @block.tensor
        def _(pe):
            def transposes(n, u):
                pe.wait_ge(xn_ready, done(n))
                pe.wait_ge(xnT_ready, done(n) - 1)
                for k in range(KD):
                    for t in range(TT):
                        mm = pe.transpose(bank[:, k, t * P:(t + 1) * P], xn[u][:, t, k * P:(k + 1) * P], ident_sb[:])
                mm.then_inc(xnT_summed, 1)

            pe.sem_inc(xnT_summed, LEAD)
            pe.wait_ge(weights_loaded, 64)
            transposes(0, 0)

            def body(pe, b, c, last):
                n, u = b * NC + c, c % 2
                pe.wait_ge(xnT_ready, done(n))
                for t in range(NT):
                    pe.wait_ge(rot_ready, n * NT + t + 1)
                    for k in range(KD):
                        mm = pe.matmul(bank[:, 2 + t, :], wqk_sb[:, k, t * P:(t + 1) * P], xnT[u][:, k, :],
                                       start=(k == 0), stop=(k == KD - 1))
                    mm.then_inc(qk_summed, 1)
                if not last:
                    transposes(n + 1, 1 - u)
                pe.wait_ge(v_ready, done(n) - 1)
                for t in range(TT):
                    for k in range(KD):
                        mm = pe.matmul(bank[:, 6 + t // 2, (t % 2) * D:(t % 2 + 1) * D],
                                       xnT[u][:, k, t * P:(t + 1) * P], wv_sb[:, k, :],
                                       start=(k == 0), stop=(k == KD - 1))
                mm.then_inc(v_summed, 1)

            over_chunks(body)(pe)

        @block.scalar
        def _(act):
            act.sem_inc(xnT_ready, LEAD)
            act.sem_inc(v_ready, LEAD)

            def spread(n):
                act.wait_ge(var_ready, n + 1)
                nc.scalar.activation(std[:], mv[:, :, 1:2], ACT.Sqrt, bias=eps[:, 0:1]).then_inc(std_ready, 1)

            def turned(n, u):
                act.wait_ge(xnT_summed, done(n))
                nc.scalar.copy(xnT[u][:], bank[:, 0:KD, :]).then_inc(xnT_ready, 1)

            def part(i, n, u, t):
                if i == 0:
                    act.wait_ge(rot_ready, (n + 1) * NT + t + 1)
                    nc.scalar.copy(parts[u][:, 0, t], rot[u][:, t]).then_inc(part0_ready, 1)
                else:
                    act.wait_ge(rest_ready, n * NT + t + 1)
                    nc.scalar.copy(parts[u][:, 1, t], rest[u][:, t]).then_inc(part1_ready, 1)

            act.wait_ge(consts_set, 3)
            spread(0)
            turned(0, 0)

            def body(act, b, c, last):
                n, u = b * NC + c, c % 2
                if not last:
                    spread(n + 1)
                act.wait_ge(parts_stored[u], 16 * 6 * halves(b, c))
                part(0, n, u, 0)
                part(0, n, u, 1)
                if not last:
                    turned(n + 1, 1 - u)
                part(0, n, u, 2)
                part(1, n, u, 0)
                act.wait_ge(v_summed, n + 1)
                act.wait_ge(v_stored[u], 16 * TT * halves(b, c))
                for a in range(2):
                    ins = nc.scalar.copy(v_sb[u][:, 2 * a:2 * a + 2, :, 0:HD],
                                         bank[:, 6 + a, :].rearrange("p (t h d) -> p t h d", t=2, h=H))
                ins.then_inc(v_ready, 1)
                part(0, n, u, 3)
                for t in range(1, NT):
                    part(1, n, u, t)

            over_chunks(body)(act)

        @block.gpsimd
        def _(pool):
            nc.gpsimd.memset(eps[:], 1e-5).then_inc(consts_set, 1)
            pool.sem_inc(part2_ready, LEAD * NT)
            for u in range(2):
                nc.gpsimd.memset(v_sb[u][:, :, :, HD:2 * HD], 1.0).then_inc(consts_set, 1)
                pool.sem_inc(parts_stored[u], 16 * 6)
                pool.sem_inc(v_stored[u], 16 * TT)

            def rests(n, u, t):
                pool.wait_ge(part0_ready, n * NT + t + 1)
                nc.gpsimd.tensor_tensor(rest[u][:, t], rot[u][:, t], parts[u][:, 0, t], ALU.subtract).then_inc(rest_ready, 1)

            def last_part(n, u, t):
                pool.wait_ge(part1_ready, n * NT + t + 1)
                nc.gpsimd.tensor_tensor(parts[u][:, 2, t], rest[u][:, t], parts[u][:, 1, t], ALU.subtract).then_inc(part2_ready, 1)

            def body(pool, b, c, last):
                n, u = b * NC + c, c % 2
                rests(n, u, 0)
                for t in range(1, NT):
                    rests(n, u, t)
                    last_part(n, u, t - 1)
                last_part(n, u, NT - 1)

            over_chunks(body)(pool)

        @block.vector
        def _(dve):
            dve.sem_inc(xn_ready, LEAD)
            dve.sem_inc(rot_ready, NT)

            def norm(n, loads, u):
                dve.wait_ge(x_loaded[u], 16 * loads)
                for t in range(TT):
                    ins = nc.vector.bn_stats(stats[:, t], x_sb[u][:, t])
                ins.then_inc(ln_step, 1)
                wait_alone(dve, ln_step, n * LN_STEPS + 1, passed)
                for t in range(TT):
                    ins = nc.vector.bn_aggr(mv[:, t], stats[:, t])
                ins.then_inc(var_ready, 1)
                dve.wait_ge(std_ready, n + 1)
                nc.vector.reciprocal(rstd[:], std[:]).then_inc(ln_step, 1)
                dve.wait_ge(ln_step, n * LN_STEPS + 2)
                dve.wait_ge(xnT_summed, two_before(n))
                for t in range(TT):
                    ins = nc.vector.tensor_scalar(xn[u][:, t], x_sb[u][:, t], mv[:, t, 0:1], rstd[:, t],
                                                  ALU.subtract, ALU.mult)
                ins.then_inc(xn_ready, 1)

            def rotate(n, u, c, t):
                a = t % 2
                dve.wait_ge(qk_summed, n * NT + t + 1)
                nc.vector.tensor_tensor(cosed[a][:], bank[:, 2 + t, :], cos_sb[:, c * CH:(c + 1) * CH],
                                        ALU.mult).then_inc(rope_step, 1)
                nc.vector.stream_shuffle(swapped[a][:], bank[:, 2 + t, :],
                                         [i ^ 1 for i in range(32)]).then_inc(rope_step, 1)
                dve.wait_ge(rope_step, n * ROPE_STEPS + 3 * t + 2)
                nc.vector.tensor_tensor(swapped[a][:], swapped[a][:], sin_sb[:, c * CH:(c + 1) * CH],
                                        ALU.mult).then_inc(rope_step, 1)
                dve.wait_ge(rope_step, n * ROPE_STEPS + 3 * t + 3)
                nc.vector.tensor_tensor(rot[u][:, t], cosed[a][:], swapped[a][:], ALU.add).then_inc(rot_ready, 1)

            norm(0, 1, 0)

            def body(dve, b, c, last):
                n, u = b * NC + c, c % 2
                if not last:
                    norm(n + 1, halves(b, c + 1), 1 - u)
                dve.wait_ge(part2_ready, two_before(n) * NT)
                for t in range(NT):
                    rotate(n, u, c, t)

            over_chunks(body)(dve)


def attend(nc, ctx, tri, bank, parts_dram, v_dram, att_dram):
    def sb(name, shape, dt=F32):
        return ctx.enter_context(nc.sbuf_tensor(name, shape, dt))

    def sem(name):
        return ctx.enter_context(nc.semaphore(name))

    q_sb = [sb(f"b_q{u}", [R * HD, JH, N], BF16) for u in range(2)]
    k_sb = [sb(f"b_k{u}", [R * HD, JH, N], BF16) for u in range(2)]
    v_sb = [sb(f"b_v{u}", [P, NKB, JH, 2 * HD]) for u in range(2)]
    tri_sb = sb("b_tri", [P, 2, P])
    PB = 8
    probs = [sb(f"b_probs{i}", [P, 2, CH]) for i in range(PB)]
    o_sb = [sb(f"b_o{i}", [P, CH]) for i in range(2)]
    sums = sb("b_sums", [P, CH])
    o_norm = [sb(f"b_on{i}", [P, CH]) for i in range(2)]

    passed = sem("b_passed")
    tri_loaded = sem("b_tri_loaded")
    qkv_loaded = [sem(f"b_qkv_loaded{u}") for u in range(2)]
    scores_summed = sem("b_scores_summed")
    probs_ready = sem("b_probs_ready")
    probs_masked = sem("b_probs_masked")
    steps_summed = sem("b_steps_summed")
    o_copied = sem("b_o_copied")
    norm_step = sem("b_norm_step")
    o_ready = sem("b_o_ready")
    o_stored = [sem(f"b_o_stored{i}") for i in range(2)]

    LOADS = 2 * R * JH + 1
    steps = [(c, kb) for c in range(NC) for kb in range((c + 1) * TT)]
    GS = len(steps)
    body_steps = [(u, c, kb) for u in range(2) for c, kb in steps]
    SB = len(body_steps)
    on_diagonal = [kb >= c * TT for _, c, kb in body_steps]
    MB = 2 * sum(on_diagonal)
    last_of_chunk = [kb == (c + 1) * TT - 1 for _, c, kb in body_steps]

    def slot(m):
        return bank[:, 2 * (m % 3):2 * (m % 3) + 2, :]

    def first_column(c, kb):
        return max(0, kb - c * TT) * P

    with nc.Block() as block:
        @block.sync
        def _(sp):
            def load(b, g, u):
                for to, picked, q in ((q_sb, QPART, 0), (k_sb, KPART, 1)):
                    for r, part in enumerate(picked):
                        for j in range(JH):
                            row = (g * JH + j) * HD
                            sp.dma_start(to[u][r * HD:(r + 1) * HD, j, :].rearrange("d (c t) -> d c t", c=NC),
                                         parts_dram[part, q, bass.ds(b * NC, NC), row:row + HD, :].rearrange("c d t -> d c t"))\
                              .then_inc(qkv_loaded[u], 16)
                sp.dma_start(v_sb[u][:].rearrange("p k j r -> p (k j r)"),
                             v_dram[bass.ds(b, 1), :, g].rearrange("o p k r -> (o p) (k r)")).then_inc(qkv_loaded[u], 16)

            def stores(b, g):
                for c in range(NC):
                    k = c % 2
                    wait_alone(sp, o_ready, done(b * NG * NC + g * NC + c), passed)
                    for j in range(JH):
                        row = (g * JH + j) * HD
                        sp.dma_start(att_dram[bass.ds(b * NC + c, 1), row:row + HD, :].rearrange("o d t -> (o d) t"),
                                     o_norm[k][j * 2 * HD:j * 2 * HD + HD, :]).then_inc(o_stored[k], 16)

            sp.dma_start(tri_sb[:], tri).then_inc(tri_loaded, 16)
            for u in range(2):
                sp.sem_inc(o_stored[u], 16 * JH)
                load(0, u, u)

            def sequence(b, last):
                for g in range(NG):
                    stores(b, g)
                    if g + 2 < NG or not last:
                        wait_alone(sp, steps_summed, (b * NG + g + 1) * GS, passed)
                        load(b + (g + 2) // NG, (g + 2) % NG, g % 2)

            with sp.Fori(0, B - 1) as b:
                sequence(b, False)
            sequence(B - 1, True)
            for k in range(2):
                sp.wait_ge(o_stored[k], 16 * JH * (B * NG * NC // 2 + 1))

        @block.tensor
        def _(pe):
            with pe.Fori(0, B * NG // 2) as i:
                def scores(m):
                    u, c, kb = body_steps[m // 2]
                    if m % (2 * GS) == 0:
                        pe.wait_ge(qkv_loaded[u], 16 * LOADS * (i + 1))
                    if m >= 3:
                        pe.wait_ge(probs_ready, i * 2 * SB + m - 2)
                    off = first_column(c, kb)
                    for h in range(2):
                        j = 2 * (m % 2) + h
                        mm = pe.matmul(slot(m)[:, h, off:CH], k_sb[u][:, j, kb * P:(kb + 1) * P],
                                       q_sb[u][:, j, c * CH + off:(c + 1) * CH], start=True, stop=True)
                    mm.then_inc(scores_summed, 1)

                def outputs(n):
                    u, c, kb = body_steps[n]
                    if on_diagonal[n]:
                        pe.wait_ge(probs_masked, i * MB + 2 * sum(on_diagonal[:n + 1]))
                    else:
                        pe.wait_ge(probs_ready, i * 2 * SB + 2 * n + 2)
                    if kb == 0:
                        pe.wait_ge(o_copied, two_before(i * 2 * NC + u * NC + c))
                    off = first_column(c, kb)
                    for j in range(JH):
                        mm = pe.matmul(bank[2 * HD * j:2 * HD * (j + 1), 6 + c % 2, off:CH], v_sb[u][:, kb, j, :],
                                       probs[(2 * n + j // 2) % PB][:, j % 2, off:CH],
                                       start=(kb == 0), stop=last_of_chunk[n])
                    mm.then_inc(steps_summed, 1)

                scores(0)
                scores(1)
                scores(2)
                for n in range(SB):
                    if n + 1 < SB:
                        scores(2 * n + 3)
                    if n >= 1:
                        outputs(n - 1)
                    if n + 2 < SB:
                        scores(2 * n + 4)
                outputs(SB - 1)

        @block.scalar
        def _(act):
            with act.Fori(0, B * NG // 2) as i:
                for m in range(2 * SB):
                    u, c, kb = body_steps[m // 2]
                    act.wait_ge(scores_summed, i * 2 * SB + m + 1)
                    if m >= PB:
                        act.wait_ge(steps_summed, i * SB + (m - PB) // 2 + 1)
                    off = first_column(c, kb)
                    nc.scalar.activation(probs[m % PB][:, :, off:CH], slot(m)[:, :, off:CH], ACT.Exp,
                                         scale=1.0 / HD).then_inc(probs_ready, 1)

        @block.gpsimd
        def _(pool):
            pool.wait_ge(tri_loaded, 16)
            with pool.Fori(0, B * NG // 2) as i:
                for m in range(2 * SB):
                    u, c, kb = body_steps[m // 2]
                    if on_diagonal[m // 2]:
                        off = first_column(c, kb)
                        pool.wait_ge(probs_ready, i * 2 * SB + m + 1)
                        nc.gpsimd.tensor_tensor(probs[m % PB][:, :, off:off + P], probs[m % PB][:, :, off:off + P],
                                                tri_sb[:], ALU.mult).then_inc(probs_masked, 1)

        @block.vector
        def _(dve):
            dve.sem_inc(o_copied, LEAD)
            dve.sem_inc(o_ready, LEAD)
            with dve.Fori(0, B * NG // 2) as i:
                for n in range(SB):
                    if not last_of_chunk[n]:
                        continue
                    u, c, _ = body_steps[n]
                    k, q = c % 2, u * NC + c
                    dve.wait_ge(steps_summed, i * SB + n + 1)
                    nc.vector.tensor_copy(o_sb[k][:], bank[:, 6 + k, :]).then_inc(o_copied, 1)
                    wait_alone(dve, o_copied, done(i * 2 * NC + q), passed)
                    nc.vector.stream_shuffle(sums[:], o_sb[k][:], [HD + r % HD for r in range(2 * HD)])\
                      .then_inc(norm_step, 1)
                    dve.wait_ge(norm_step, i * 4 * NC + 2 * q + 1)
                    nc.vector.reciprocal(sums[:], sums[:]).then_inc(norm_step, 1)
                    dve.wait_ge(norm_step, i * 4 * NC + 2 * q + 2)
                    dve.wait_ge(o_stored[k], 16 * JH * (i * NC + q // 2 + 1))
                    nc.vector.tensor_tensor(o_norm[k][:], o_sb[k][:], sums[:], ALU.mult).then_inc(o_ready, 1)


def experts(nc, ctx, x, wo, bo, w1, b1, w2, b2, cent, wr, ident_sb, bank, att_dram, out):
    def sb(name, shape, dt=F32):
        return ctx.enter_context(nc.sbuf_tensor(name, shape, dt))

    def sem(name):
        return ctx.enter_context(nc.semaphore(name))

    wo_sb = sb("c_wo", [P, KD, D])
    bo_sb = sb("c_bo", [P, TT, D])
    w1_sb = sb("c_w1", [P, KD, E, F])
    b1_sb = sb("c_b1", [P, E])
    w2_sb = sb("c_w2", [P, E, D])
    b2_sb = sb("c_b2", [E, D])
    cent_sb = sb("c_cent", [E, D])
    cent_sq = sb("c_cent_sq", [E, D])
    cent_n = sb("c_cent_n", [E, 1])
    cent_s = sb("c_cent_s", [E, 1])
    wr_sb = sb("c_wr", [E, D])
    route = sb("c_route", [P, KD, 2 * E])
    minus_half = sb("c_minus_half", [P, TT])
    half = sb("c_half", [P, TT])
    att_sb = [sb(f"c_att{u}", [P, KD, CH]) for u in range(2)]
    x_sb = [sb(f"c_x{u}", [P, TT, D]) for u in range(2)]
    x2 = [sb(f"c_x2{u}", [P, TT, D]) for u in range(2)]
    xn = [sb(f"c_xn{u}", [P, TT, D]) for u in range(2)]
    xnT = [sb(f"c_xnT{u}", [P, KD, CH]) for u in range(2)]
    stats = sb("c_stats", [P, TT, 6])
    mv = sb("c_mv", [P, TT, 2])
    var_eps = sb("c_var_eps", [P, TT])
    rstd = sb("c_rstd", [P, TT])
    sq = sb("c_sq", [P, TT])
    root = sb("c_root", [P, TT])
    length = [sb(f"c_length{u}", [P, TT]) for u in range(2)]
    scored = sb("c_scored", [P, TT, 2 * E])
    logits = sb("c_logits", [P, TT, E])
    top = sb("c_top", [P, TT, 8])
    shifted = sb("c_shifted", [P, TT, E])
    kept = sb("c_kept", [P, TT, E])
    exps = sb("c_exps", [P, TT, E])
    total = sb("c_total", [P, TT])
    gates = [sb(f"c_gates{u}", [P, TT, E]) for u in range(2)]
    gatesT = sb("c_gatesT", [E, CH])
    hid = [sb(f"c_hid{u}", [P, E, CH]) for u in range(2)]
    acc = [sb(f"c_acc{u}", [P, TT, D]) for u in range(2)]
    y = [sb(f"c_y{u}", [P, TT, D]) for u in range(2)]

    passed = sem("c_passed")
    weights_loaded = sem("c_weights_loaded")
    att_loaded = [sem(f"c_att_loaded{u}") for u in range(2)]
    out_stored = [sem(f"c_out_stored{u}") for u in range(2)]
    consts_set = sem("c_consts_set")
    cent_step = sem("c_cent_step")
    cent_rooted = sem("c_cent_rooted")
    routeT_summed = sem("c_routeT_summed")
    route_ready = sem("c_route_ready")
    o_summed = sem("c_o_summed")
    x2_ready = sem("c_x2_ready")
    ln_step = sem("c_ln_step")
    var_ready = sem("c_var_ready")
    rstd_ready = sem("c_rstd_ready")
    xn_ready = sem("c_xn_ready")
    xnT_summed = sem("c_xnT_summed")
    xnT_ready = sem("c_xnT_ready")
    scores_summed = sem("c_scores_summed")
    gate_step = sem("c_gate_step")
    exps_ready = sem("c_exps_ready")
    gates_ready = sem("c_gates_ready")
    gatesT_summed = sem("c_gatesT_summed")
    gatesT_ready = sem("c_gatesT_ready")
    hid_summed = sem("c_hid_summed")
    hid_ready = sem("c_hid_ready")
    y_summed = sem("c_y_summed")
    y_added = sem("c_y_added")

    YB = (E + 1) * TT // 2
    GATE_STAGES = 10
    WEIGHTS = 8 + TT

    with nc.Block() as block:
        def over_chunks(body):
            def run(eng):
                with eng.Fori(0, NCH // 2 - 1) as i:
                    body(eng, i, 0, False)
                    body(eng, i, 1, False)
                body(eng, NCH // 2 - 1, 0, False)
                body(eng, NCH // 2 - 1, 1, True)
            return run

        @block.sync
        def _(sp):
            def load(n, u):
                sp.dma_start(att_sb[u][:], att_dram[bass.ds(n, 1)].rearrange("o (k p) t -> p (o k) t", p=P))\
                  .then_inc(att_loaded[u], 16)
                sp.dma_start(x_sb[u][:], x[bass.ds(n * CH, CH), :].rearrange("(t p) d -> p t d", p=P))\
                  .then_inc(att_loaded[u], 16)

            weights = [(cent_sb[:], cent), (wr_sb[:], wr), (wo_sb[:], wo.rearrange("(k p) n -> p k n", p=P)),
                       (w1_sb[:, 0], w1[:, 0:P, :].rearrange("e p f -> p e f")),
                       (w1_sb[:, 1], w1[:, P:D, :].rearrange("e p f -> p e f")), (b1_sb[:], b1),
                       (w2_sb[:], w2.rearrange("e f d -> f e d")), (b2_sb[:], b2)]
            weights += [(bo_sb[:, t], bo.partition_broadcast(P)) for t in range(TT)]
            for k, (to, source) in enumerate(weights):
                sp.dma_start(to, source).then_inc(weights_loaded, 16)
            load(0, 0)
            load(1, 1)

            def body(sp, i, u, last):
                n = 2 * i + u
                if not isinstance(i, int):
                    wait_alone(sp, x2_ready, done(n), passed)
                    load(n + 2, u)
                wait_alone(sp, y_added, (done(n)) * YB, passed)
                sp.dma_start(out[bass.ds(n * CH, CH), :].rearrange("(t p) d -> p t d", p=P), y[u][:])\
                  .then_inc(out_stored[u], 16)

            over_chunks(body)(sp)
            for u in range(2):
                sp.wait_ge(out_stored[u], 16 * (NCH // 2 + 1))

        @block.tensor
        def _(pe):
            def projected(n, i, u):
                pe.wait_ge(att_loaded[u], 32 * (i + 1))
                pe.wait_ge(gates_ready, done(n) - 1)
                pe.wait_ge(gatesT_ready, two_before(n))
                for t in range(TT):
                    for k in range(KD):
                        mm = pe.matmul(bank[:, 2 + t // 2, (t % 2) * D:(t % 2 + 1) * D],
                                       att_sb[u][:, k, t * P:(t + 1) * P], wo_sb[:, k, :],
                                       start=(k == 0), stop=(k == KD - 1))
                mm.then_inc(o_summed, 1)

            def turned(n, u):
                pe.wait_ge(xn_ready, done(n))
                pe.wait_ge(xnT_ready, done(n) - 1)
                for k in range(KD):
                    for t in range(TT):
                        mm = pe.transpose(bank[:, 4 + k, t * P:(t + 1) * P], xn[u][:, t, k * P:(k + 1) * P], ident_sb[:])
                mm.then_inc(xnT_summed, 1)

            def routed(n, u):
                pe.wait_ge(xnT_ready, done(n))
                for t in range(TT):
                    for k in range(KD):
                        mm = pe.matmul(bank[:, 2, t * 2 * E:(t + 1) * 2 * E], xnT[u][:, k, t * P:(t + 1) * P],
                                       route[:, k, :], start=(k == 0), stop=(k == KD - 1))
                mm.then_inc(scores_summed, 1)

            pe.sem_inc(xnT_summed, LEAD)
            pe.wait_ge(weights_loaded, 16 * WEIGHTS)
            pe.wait_ge(cent_step, 4)
            for k in range(KD):
                pe.transpose(bank[:, 4, k * 2 * E:k * 2 * E + E], cent_sb[:, k * P:(k + 1) * P], ident_sb[0:E, 0:E])
                mm = pe.transpose(bank[:, 4, k * 2 * E + E:(k + 1) * 2 * E], wr_sb[:, k * P:(k + 1) * P], ident_sb[0:E, 0:E])
            mm.then_inc(routeT_summed, 1)
            pe.wait_ge(route_ready, 1)
            projected(0, 0, 0)
            turned(0, 0)
            routed(0, 0)

            def body(pe, i, u, last):
                n = 2 * i + u
                if not last:
                    projected(n + 1, i + u, 1 - u)
                for e in range(E):
                    pe.wait_ge(hid_ready, n * E + e - 1 + LEAD * E)
                    for k in range(KD):
                        mm = pe.matmul(bank[:, e % 2, :], w1_sb[:, k, e, :], xnT[u][:, k, :],
                                       start=(k == 0), stop=(k == KD - 1))
                    mm.then_inc(hid_summed, 1)
                if not last:
                    turned(n + 1, 1 - u)
                pe.wait_ge(gates_ready, done(n))
                for t in range(TT):
                    mm = pe.transpose(bank[0:E, 3, t * P:(t + 1) * P], gates[u][:, t, :], ident_sb[:])
                mm.then_inc(gatesT_summed, 1)
                for e in range(E):
                    if e == 1 and not last:
                        routed(n + 1, 1 - u)
                    pe.wait_ge(hid_ready, n * E + e + 1 + LEAD * E)
                    for t in range(TT):
                        m = e * TT // 2 + t // 2
                        if t % 2 == 0:
                            pe.wait_ge(y_added, n * YB + m - 2 + LEAD * YB + 1)
                        mm = pe.matmul(bank[:, 6 + m % 2, (t % 2) * D:(t % 2 + 1) * D],
                                       hid[u][:, e, t * P:(t + 1) * P], w2_sb[:, e, :], start=True, stop=True)
                        if t % 2 == 1:
                            mm.then_inc(y_summed, 1)
                pe.wait_ge(gatesT_ready, done(n))
                for t in range(TT):
                    m = E * TT // 2 + t // 2
                    if t % 2 == 0:
                        pe.wait_ge(y_added, n * YB + m - 2 + LEAD * YB + 1)
                    mm = pe.matmul(bank[:, 6 + m % 2, (t % 2) * D:(t % 2 + 1) * D],
                                   gatesT[:, t * P:(t + 1) * P], b2_sb[:], start=True, stop=True)
                    if t % 2 == 1:
                        mm.then_inc(y_summed, 1)

            over_chunks(body)(pe)

        @block.scalar
        def _(act):
            act.sem_inc(xnT_ready, LEAD)
            act.sem_inc(hid_ready, LEAD * E)
            act.sem_inc(gatesT_ready, LEAD)

            def turned(n, u):
                act.wait_ge(xnT_summed, done(n))
                nc.scalar.copy(xnT[u][:], bank[:, 4:4 + KD, :]).then_inc(xnT_ready, 1)

            def exped(n):
                act.wait_ge(gate_step, n * GATE_STAGES + 6)
                nc.scalar.activation(exps[:], shifted[:], ACT.Exp).then_inc(exps_ready, 1)

            act.wait_ge(weights_loaded, 16 * WEIGHTS)
            turned(0, 0)
            exped(0)

            def body(act, i, u, last):
                n = 2 * i + u
                for e in range(E):
                    act.wait_ge(hid_summed, n * E + e + 1)
                    nc.scalar.activation(hid[u][:, e, :], bank[:, e % 2, :], ACT.Gelu, bias=b1_sb[:, e:e + 1])\
                      .then_inc(hid_ready, 1)
                if not last:
                    turned(n + 1, 1 - u)
                act.wait_ge(gatesT_summed, n + 1)
                nc.scalar.copy(gatesT[:], bank[0:E, 3, :]).then_inc(gatesT_ready, 1)
                if not last:
                    exped(n + 1)

            over_chunks(body)(act)

        @block.gpsimd
        def _(pool):
            nc.gpsimd.memset(minus_half[:], -0.5).then_inc(consts_set, 1)
            nc.gpsimd.memset(half[:], 0.5).then_inc(consts_set, 1)
            pool.wait_ge(consts_set, 2)
            pool.wait_ge(cent_step, 2)
            nc.gpsimd.tensor_tensor(cent_s[:], cent_n[:], half[0:E, 0:1], ALU.pow).then_inc(cent_rooted, 1)

            def roots(n):
                pool.wait_ge(var_ready, n + 1)
                nc.gpsimd.tensor_tensor(root[:], sq[:], half[:], ALU.pow).then_inc(rstd_ready, 1)
                nc.gpsimd.tensor_tensor(rstd[:], var_eps[:], minus_half[:], ALU.pow).then_inc(rstd_ready, 1)

            with pool.Fori(0, NCH) as n:
                roots(n)

        @block.vector
        def _(dve):
            dve.sem_inc(x2_ready, LEAD)
            dve.sem_inc(xn_ready, LEAD)
            dve.sem_inc(gates_ready, LEAD)
            dve.sem_inc(y_added, LEAD * YB)
            for u in range(2):
                dve.sem_inc(out_stored[u], 16)
            dve.wait_ge(weights_loaded, 16 * WEIGHTS)
            nc.vector.tensor_tensor(cent_sq[:], cent_sb[:], cent_sb[:], ALU.mult).then_inc(cent_step, 1)
            dve.wait_ge(cent_step, 1)
            nc.vector.tensor_reduce(cent_n[:], cent_sq[:], AX.X, ALU.add).then_inc(cent_step, 1)
            dve.wait_ge(cent_rooted, 1)
            nc.vector.tensor_scalar(cent_s[:], cent_s[:], 1e-12, None, ALU.max).then_inc(cent_rooted, 1)
            dve.wait_ge(cent_rooted, 2)
            nc.vector.reciprocal(cent_n[:], cent_s[:]).then_inc(cent_step, 1)
            dve.wait_ge(cent_step, 3)
            nc.vector.tensor_scalar(cent_sb[:], cent_sb[:], cent_n[:, 0:1], None, ALU.mult).then_inc(cent_step, 1)
            dve.wait_ge(routeT_summed, 1)
            nc.vector.tensor_copy(route[:], bank[:, 4, 0:KD * 2 * E].rearrange("p (k e) -> p k e", k=KD))\
              .then_inc(route_ready, 1)

            def norm(n, i, u):
                dve.wait_ge(att_loaded[u], 32 * (i + 1))
                nc.vector.tensor_tensor(x2[u][:], x_sb[u][:], bo_sb[:], ALU.add).then_inc(ln_step, 1)
                dve.wait_ge(ln_step, n * 3 + 1)
                dve.wait_ge(o_summed, n + 1)
                nc.vector.tensor_tensor(x2[u][:], bank[:, 2:4, :].rearrange("p a (b d) -> p (a b) d", b=2), x2[u][:],
                                        ALU.add).then_inc(x2_ready, 1)
                dve.wait_ge(x2_ready, done(n))
                for t in range(TT):
                    ins = nc.vector.bn_stats(stats[:, t], x2[u][:, t])
                ins.then_inc(ln_step, 1)
                wait_alone(dve, ln_step, n * 3 + 2, passed)
                for t in range(TT):
                    ins = nc.vector.bn_aggr(mv[:, t], stats[:, t])
                ins.then_inc(ln_step, 1)
                dve.wait_ge(ln_step, n * 3 + 3)
                nc.vector.tensor_scalar(sq[:], mv[:, :, 1], float(D), None, ALU.mult)
                nc.vector.tensor_scalar(var_eps[:], mv[:, :, 1], 1e-5, None, ALU.add).then_inc(var_ready, 1)
                dve.wait_ge(rstd_ready, 2 * (n + 1))
                dve.wait_ge(xnT_summed, two_before(n))
                nc.vector.tensor_tensor(length[u][:], root[:], rstd[:], ALU.mult)
                for t in range(TT):
                    ins = nc.vector.tensor_scalar(xn[u][:, t], x2[u][:, t], mv[:, t, 0:1], rstd[:, t:t + 1],
                                                  ALU.subtract, ALU.mult)
                ins.then_inc(xn_ready, 1)

            def gate(n, u, stage):
                def link(ins):
                    ins.then_inc(gate_step, 1)

                if stage == 4:
                    wait_alone(dve, gate_step, n * GATE_STAGES + stage, passed)
                elif stage > 0:
                    dve.wait_ge(gate_step, n * GATE_STAGES + stage)
                if stage == 0:
                    dve.wait_ge(xn_ready, done(n))
                    link(nc.vector.tensor_scalar(length[u][:], length[u][:], 1e-12, None, ALU.max))
                if stage == 1:
                    link(nc.vector.reciprocal(length[u][:], length[u][:]))
                if stage == 2:
                    dve.wait_ge(scores_summed, n + 1)
                    link(nc.vector.tensor_copy(scored[:], bank[:, 2, 0:TT * 2 * E].rearrange("p (t e) -> p t e", t=TT)))
                if stage == 3:
                    for t in range(TT):
                        ins = nc.vector.scalar_tensor_tensor(out=logits[:, t], in0=scored[:, t, 0:E],
                                                             scalar=length[u][:, t:t + 1],
                                                             in1=scored[:, t, E:2 * E], op0=ALU.mult, op1=ALU.add)
                    link(ins)
                if stage == 4:
                    for t in range(TT):
                        ins = nc.vector.max(top[:, t], logits[:, t])
                    link(ins)
                if stage == 5:
                    link(nc.vector.tensor_tensor(shifted[:], logits[:], top[:, :, 0:1].to_broadcast([P, TT, E]),
                                                 ALU.subtract))
                if stage == 6:
                    link(nc.vector.tensor_tensor(kept[:], logits[:], top[:, :, 1:2].to_broadcast([P, TT, E]), ALU.is_ge))
                if stage == 7:
                    dve.wait_ge(exps_ready, n + 1)
                    link(nc.vector.tensor_tensor(kept[:], kept[:], exps[:], ALU.mult))
                if stage == 8:
                    link(nc.vector.tensor_reduce(total[:], kept[:], AX.X, ALU.add))
                if stage == 9:
                    link(nc.vector.reciprocal(total[:], total[:]))
                if stage == 10:
                    nc.vector.tensor_tensor(gates[u][:], kept[:], total[:].unsqueeze(2).to_broadcast([P, TT, E]),
                                            ALU.mult).then_inc(gates_ready, 1)

            def add(n, i, u, m):
                e, a = m // 2, m % 2
                dve.wait_ge(y_summed, n * YB + m + 1)
                if m >= 2:
                    dve.wait_ge(y_added, n * YB + m - 1 + LEAD * YB)
                if e < E:
                    for t in (2 * a, 2 * a + 1):
                        ins = nc.vector.scalar_tensor_tensor(
                            out=acc[u][:, t], in0=bank[:, 6 + m % 2, (t % 2) * D:(t % 2 + 1) * D],
                            scalar=gates[u][:, t, e:e + 1], in1=(x2 if e == 0 else acc)[u][:, t],
                            op0=ALU.mult, op1=ALU.add)
                else:
                    if a == 0:
                        dve.wait_ge(out_stored[u], 16 * (i + 1))
                    ins = nc.vector.tensor_tensor(y[u][:, 2 * a:2 * a + 2],
                                                  bank[:, 6 + m % 2, :].rearrange("p (b d) -> p b d", b=2),
                                                  acc[u][:, 2 * a:2 * a + 2], ALU.add)
                ins.then_inc(y_added, 1)

            norm(0, 0, 0)
            for stage in range(GATE_STAGES + 1):
                gate(0, 0, stage)

            def body(dve, i, u, last):
                n = 2 * i + u
                if not last:
                    norm(n + 1, i + u, 1 - u)
                dve.wait_ge(gates_ready, done(n))
                for m in range(YB):
                    add(n, i, u, m)
                    if not last and 0 <= m - 6 <= GATE_STAGES:
                        gate(n + 1, 1 - u, m - 6)

            over_chunks(body)(dve)


def kernel(**inputs):
    import numpy as np
    import concourse.bacc as bacc
    from concourse.bass_utils import run_bass_kernel_spmd

    def f(name):
        return np.asarray(inputs[name])

    inv_freq = (np.float32(1.0) / np.power(np.float32(10000.0), np.arange(0, HD, 2, dtype=np.float32) / np.float32(HD)))
    angle = np.arange(N, dtype=np.float32)[:, None] * inv_freq.astype(np.float32)[None, :]
    row = np.arange(P) % HD // 2
    cos = np.cos(angle).astype(np.float32).T[row]
    sin = np.sin(angle).astype(np.float32).T[row] * np.where(np.arange(P) % 2 == 0, -1, 1).astype(np.float32)[:, None]
    tri = (np.arange(P)[None, :] >= np.arange(P)[:, None]).astype(np.float32)
    arrays = {
        "x": f("L0_attn_x").reshape(B * N, D),
        "wqk": np.concatenate([f("L0_attn_Wq").T, f("L0_attn_Wk").T], axis=1),
        "wv": f("L0_attn_Wv").T, "wo": f("L0_attn_Wo").T, "bo": f("L0_attn_bo").reshape(1, D),
        "w1": f("L0_ffn_w1"), "b1": f("L0_ffn_b1").T, "w2": f("L0_ffn_w2"), "b2": f("L0_ffn_b2"),
        "cent": f("L0_ffn_centroids"), "wr": f("L0_ffn_w_route"),
        "cos": cos, "sin": sin, "tri": np.stack([tri, tri], axis=1), "ident": np.eye(P, dtype=np.float32),
    }
    arrays = {k: np.ascontiguousarray(a) for k, a in arrays.items()}
    nc = bacc.Bacc("TRN2", target_bir_lowering=False, num_devices=1)
    aps = {k: nc.dram_tensor(k, a.shape, mybir.dt.from_np(a.dtype), kind="ExternalInput").ap() for k, a in arrays.items()}
    out = nc.dram_tensor("out", (B * N, D), F32, kind="ExternalOutput").ap()
    layer_kernel(nc, **aps, out=out)
    r = run_bass_kernel_spmd(nc, [arrays], core_ids=[0])
    return r.results[0]["out"].reshape(B, N, D)
```

```python
from contextlib import ExitStack

import concourse.bass as bass
from concourse import mybir

F32 = mybir.dt.float32
BF16 = mybir.dt.bfloat16
F32R = mybir.dt.float32r
I32 = mybir.dt.int32
ALU = mybir.AluOpType
ACT = mybir.ActivationFunctionType
AX = mybir.AxisListType

P = 128
B, N, D = 4, 2048, 256
H, HD = 16, 16
E, F = 8, 128
CH = 512
NC = N // CH
NCH = B * NC
TT = CH // P
KD = D // P
JH = 4
NG = H // JH
NKB = N // P
R = 6
QPART = (0, 0, 1, 1, 0, 2)
KPART = (0, 1, 0, 1, 2, 0)
PRODUCTS = ((0, 0), (0, 1), (1, 0))
SCORE_BOUND = 60.0
WEIGHT_BOUND = 1e6
LEAD = 2


def done(n):
    return n + 1 + LEAD


def two_before(n):
    return n - 1 + LEAD


def wait_alone(eng, semaphore, value, passed):
    eng.wait_ge(semaphore, value)
    eng.sem_inc(passed, 1)


def where(eng, flag, value):
    return eng.If(eng.value_load(flag[0:1, 0:1], min_val=0, max_val=1) == value)


def layer_kernel(nc, x, wqkv, wo, bo, w1, b1, w2, b2, cent, wr, cos, sin, tri, causal, head_mask, ident, out):
    ctx = ExitStack()
    with ctx:
        def sb(name, shape, dt=F32):
            return ctx.enter_context(nc.sbuf_tensor(name, shape, dt))

        def sem(name):
            return ctx.enter_context(nc.semaphore(name))

        parts_dram = nc.dram_tensor("parts_dram", (3, 2, B, D, N), BF16, kind="Internal").ap()
        v_dram = nc.dram_tensor("v_dram", (B, P, NG, NKB, JH * 2 * HD), F32, kind="Internal").ap()
        att_dram = nc.dram_tensor("att_dram", (NCH, D, CH), F32, kind="Internal").ap()

        bank = ctx.enter_context(nc.psum_tensor("bank", [P, 8, CH], F32))

        ident_sb = sb("ident_sb", [P, P])
        load_const(nc, ctx, sb, sem, ident, ident_sb)
        bounded = sb("bounded", [1, 1], I32)
        with ExitStack() as s1:
            project(nc, s1, x, wqkv, cos, sin, head_mask, ident_sb, bank, parts_dram, v_dram, bounded)
        with ExitStack() as s2:
            attend(nc, s2, tri, bounded, bank, parts_dram, v_dram, att_dram)
        with ExitStack() as s3:
            attend_unbounded(nc, s3, causal, bounded, ident_sb, bank, parts_dram, v_dram, att_dram)
        with ExitStack() as s4:
            experts(nc, s4, x, wo, bo, w1, b1, w2, b2, cent, wr, ident_sb, bank, att_dram, out)


def load_const(nc, ctx, sb, sem, ident, ident_sb):
    loaded = sem("ident_loaded")
    with nc.Block() as block:
        @block.sync
        def _(sp):
            sp.dma_start(ident_sb[:], ident).then_inc(loaded, 16)
            sp.wait_ge(loaded, 16)


def project(nc, ctx, x, wqkv, cos, sin, head_mask, ident_sb, bank, parts_dram, v_dram, bounded):
    def sb(name, shape, dt=F32):
        return ctx.enter_context(nc.sbuf_tensor(name, shape, dt))

    def sem(name):
        return ctx.enter_context(nc.semaphore(name))

    NT = 2 * KD
    w_in = sb("a_w_in", [P, KD, 3 * D])
    w = [sb(f"a_w{i}", [P, KD, 3 * D], F32R) for i in range(2)]
    cos_sb = sb("cos_sb", [P, N])
    sin_sb = sb("sin_sb", [P, N])
    x_sb = [sb(f"a_x{u}", [P, TT, D]) for u in range(2)]
    xn = [sb(f"a_xn{u}", [P, TT, D]) for u in range(2)]
    xnT = [[sb(f"a_xnT{u}{i}", [P, KD, CH], F32R) for i in range(2)] for u in range(2)]
    stats = sb("a_stats", [P, TT, 6])
    mv = sb("a_mv", [P, TT, 2])
    std = sb("a_std", [P, TT, 1])
    rstd = sb("a_rstd", [P, TT, 1])
    shift = sb("a_shift", [P, TT, 1])
    eps = sb("a_eps", [P, 1])
    cosed = [sb(f"a_cosed{q}", [P, KD, CH]) for q in range(2)]
    swapped = [sb(f"a_swapped{q}", [P, KD, CH]) for q in range(2)]
    rot = [sb(f"a_rot{u}", [P, NT, CH]) for u in range(2)]
    rest = sb("a_rest", [P, NT, CH])
    parts = [sb(f"a_parts{u}", [P, 3, NT, CH], BF16) for u in range(2)]
    v_sb = [sb(f"a_v{u}", [P, TT, H, 2 * HD]) for u in range(2)]

    head_sb = sb("a_head_mask", [P, P])
    gram = sb("a_gram", [P, NT, P])
    row_sums = sb("a_row_sums", [P, NT])
    limits = sb("a_limits", [P, 3])
    largest = sb("a_largest", [1, 3])
    within = sb("a_within", [1, 2])

    passed = sem("a_passed")
    head_loaded = sem("a_head_loaded")
    gram_summed = sem("a_gram_summed")
    gram_step = sem("a_gram_step")
    limits_turned = sem("a_limits_turned")
    weights_loaded = sem("a_weights_loaded")
    x_loaded = [sem(f"a_x_loaded{u}") for u in range(2)]
    parts_stored = [sem(f"a_parts_stored{u}") for u in range(2)]
    v_stored = [sem(f"a_v_stored{u}") for u in range(2)]
    consts_set = sem("a_consts_set")
    ln_step = sem("a_ln_step")
    var_ready = sem("a_var_ready")
    std_ready = sem("a_std_ready")
    shift_ready = sem("a_shift_ready")
    halves_ready = sem("a_halves_ready")
    xn_ready = sem("a_xn_ready")
    xnT_summed = sem("a_xnT_summed")
    xnT_high_ready = sem("a_xnT_high_ready")
    xnT_ready = sem("a_xnT_ready")
    w_high_ready = sem("a_w_high_ready")
    w_ready = sem("a_w_ready")
    qk_summed = sem("a_qk_summed")
    v_summed = sem("a_v_summed")
    v_ready = sem("a_v_ready")
    q_step = sem("a_q_step")
    qk_read = [sem("a_q_read"), sem("a_k_read")]
    rope_step = sem("a_rope_step")
    rot_ready = [sem("a_q_rot_ready"), sem("a_k_rot_ready")]
    part0_ready = sem("a_part0_ready")
    rest_ready = sem("a_rest_ready")
    part1_ready = sem("a_part1_ready")
    part2_ready = sem("a_part2_ready")

    LN_STEPS, ROPE_STEPS = 2, 2

    def over_chunks(body):
        def run(eng):
            with eng.Fori(0, B - 1) as b:
                for c in range(NC):
                    body(eng, b, c, NC)
            for c in range(NC):
                body(eng, B - 1, c, NC - 1 - c)
        return run

    def halves(b, c):
        return b * (NC // 2) + c // 2 + 1

    with nc.Block() as block:
        @block.sync
        def _(sp):
            def load_x(n, u):
                sp.dma_start(x_sb[u][:], x[bass.ds(n * CH, CH), :].rearrange("(t p) d -> p t d", p=P))\
                  .then_inc(x_loaded[u], 16)

            load_x(0, 0)
            sp.dma_start(w_in[:], wqkv.rearrange("(k p) n -> p k n", p=P)).then_inc(weights_loaded, 16)
            sp.dma_start(cos_sb[:], cos).then_inc(weights_loaded, 16)
            sp.dma_start(sin_sb[:], sin).then_inc(weights_loaded, 16)
            load_x(1, 1)
            sp.dma_start(head_sb[:], head_mask).then_inc(head_loaded, 16)
            sp.wait_ge(xn_ready, 1 + LEAD)
            load_x(2, 0)

            def body(sp, b, c, ahead):
                n, u = b * NC + c, c % 2
                if ahead >= 3:
                    wait_alone(sp, xn_ready, done(n) + 1, passed)
                    load_x(n + 3, 1 - u)
                wait_alone(sp, v_ready, done(n), passed)
                for t in range(TT):
                    sp.dma_start(v_dram[bass.ds(b, 1), :, :, c * TT + t, :].rearrange("o p g r -> p (o g) r"),
                                 v_sb[u][:, t].rearrange("p (g j) r -> p g (j r)", g=NG)).then_inc(v_stored[u], 16)
                for q in range(2):
                    wait_alone(sp, part2_ready, done(n) * 2 - 1 + q, passed)
                    for i in range(3):
                        sp.dma_start(parts_dram[i, q, bass.ds(b, 1), :, c * CH:(c + 1) * CH]
                                     .rearrange("o (k p) t -> p (o k) t", p=P),
                                     parts[u][:, i, KD * q:KD * (q + 1)]).then_inc(parts_stored[u], 16)

            over_chunks(body)(sp)
            for u in range(2):
                sp.wait_ge(v_stored[u], 16 * TT * (NCH // 2 + 1))
                sp.wait_ge(parts_stored[u], 16 * 6 * (NCH // 2 + 1))

        @block.tensor
        def _(pe):
            def transposes(n, u):
                pe.wait_ge(xn_ready, done(n))
                pe.wait_ge(xnT_ready, done(n) - 1)
                for k in range(KD):
                    for t in range(TT):
                        mm = pe.transpose(bank[:, k, t * P:(t + 1) * P], xn[u][:, t, k * P:(k + 1) * P], ident_sb[:])
                mm.then_inc(xnT_summed, 1)

            pe.sem_inc(xnT_summed, LEAD)
            pe.wait_ge(weights_loaded, 48)
            for t in range(NT):
                for k in range(KD):
                    mm = pe.matmul(bank[:, 2 + t, 0:P], w_in[:, k, t * P:(t + 1) * P], w_in[:, k, t * P:(t + 1) * P],
                                   start=(k == 0), stop=(k == KD - 1))
            mm.then_inc(gram_summed, 1)
            transposes(0, 0)
            pe.wait_ge(w_ready, 1)
            pe.wait_ge(gram_step, 1)

            def body(pe, b, c, ahead):
                n, u = b * NC + c, c % 2
                pe.wait_ge(xnT_ready, done(n))
                for t in range(NT):
                    if t % KD == 0:
                        pe.wait_ge(qk_read[t // KD], n + 1)
                    for k in range(KD):
                        for i, (a, z) in enumerate(PRODUCTS):
                            mm = pe.matmul(bank[:, 2 + t, :], w[a][:, k, t * P:(t + 1) * P], xnT[u][z][:, k, :],
                                           start=(k + i == 0), stop=(k == KD - 1 and i == 2))
                    if t % KD == KD - 1:
                        mm.then_inc(qk_summed, 1)
                    if t == KD - 1 and ahead >= 1:
                        transposes(n + 1, 1 - u)
                pe.wait_ge(v_ready, done(n) - 1)
                for t in range(TT):
                    for k in range(KD):
                        for i, (a, z) in enumerate(PRODUCTS):
                            mm = pe.matmul(bank[:, 6 + t // 2, (t % 2) * D:(t % 2 + 1) * D],
                                           xnT[u][a][:, k, t * P:(t + 1) * P], w[z][:, k, 2 * D:3 * D],
                                           start=(k + i == 0), stop=(k == KD - 1 and i == 2))
                mm.then_inc(v_summed, 1)

            over_chunks(body)(pe)
            pe.wait_ge(gram_step, 4)
            for j in range(3):
                mm = pe.transpose(bank[0:1, 0, j * P:(j + 1) * P], limits[:, j:j + 1], ident_sb[:])
            mm.then_inc(limits_turned, 1)

        @block.scalar
        def _(act):
            act.sem_inc(v_ready, LEAD)
            act.sem_inc(xn_ready, LEAD)
            act.wait_ge(weights_loaded, 48)
            nc.scalar.copy(w[0][:], w_in[:]).then_inc(w_high_ready, 1)

            def spread(n):
                act.wait_ge(var_ready, n + 1)
                nc.scalar.activation(std[:], mv[:, :, 1:2], ACT.Sqrt, bias=eps[:, 0:1]).then_inc(std_ready, 1)

            def normed(n, u):
                act.wait_ge(shift_ready, n + 1)
                act.wait_ge(xnT_summed, two_before(n))
                for t in range(TT):
                    ins = nc.scalar.activation(xn[u][:, t], x_sb[u][:, t], ACT.Identity, bias=shift[:, t],
                                               scale=rstd[:, t])
                ins.then_inc(xn_ready, 1)

            def turned(n, u):
                act.wait_ge(xnT_summed, done(n))
                nc.scalar.copy(xnT[u][0][:], bank[:, 0:KD, :]).then_inc(xnT_high_ready, 1)

            def part(i, n, u, q):
                of = slice(KD * q, KD * (q + 1))
                if i == 0:
                    act.wait_ge(rot_ready[q], n + 2)
                    nc.scalar.copy(parts[u][:, 0, of], rot[u][:, of]).then_inc(part0_ready, 1)
                else:
                    act.wait_ge(rest_ready, n * 2 + q + 1)
                    nc.scalar.copy(parts[u][:, 1, of], rest[:, of]).then_inc(part1_ready, 1)

            def q_parts(n, u, earlier):
                act.wait_ge(parts_stored[u], 16 * 6 * earlier)
                part(0, n, u, 0)

            act.wait_ge(consts_set, 3)
            spread(0)
            normed(0, 0)
            spread(1)
            turned(0, 0)
            normed(1, 1)
            spread(2)
            turned(1, 1)
            q_parts(0, 0, 1)
            part(1, 0, 0, 0)

            def body(act, b, c, ahead):
                n, u = b * NC + c, c % 2
                if ahead >= 2:
                    normed(n + 2, u)
                act.wait_ge(v_summed, n + 1)
                act.wait_ge(v_stored[u], 16 * TT * halves(b, c))
                for a in range(2):
                    ins = nc.scalar.copy(v_sb[u][:, 2 * a:2 * a + 2, :, 0:HD],
                                         bank[:, 6 + a, :].rearrange("p (t h d) -> p t h d", t=2, h=H))
                ins.then_inc(v_ready, 1)
                part(0, n, u, 1)
                part(1, n, u, 1)
                if ahead >= 3:
                    spread(n + 3)
                if ahead >= 2:
                    turned(n + 2, u)
                if ahead >= 1:
                    q_parts(n + 1, 1 - u, halves(b, c + 1))
                    part(1, n + 1, 1 - u, 0)

            over_chunks(body)(act)

        @block.gpsimd
        def _(pool):
            nc.gpsimd.memset(eps[:], 1e-5).then_inc(consts_set, 1)
            pool.sem_inc(part2_ready, LEAD * 2)
            pool.sem_inc(rot_ready[1], 1)
            for u in range(2):
                nc.gpsimd.memset(v_sb[u][:, :, :, HD:2 * HD], 1.0).then_inc(consts_set, 1)
                pool.sem_inc(parts_stored[u], 16 * 6)
                pool.sem_inc(v_stored[u], 16 * TT)

            def rests(n, u, q):
                of = slice(KD * q, KD * (q + 1))
                pool.wait_ge(part0_ready, n * 2 + q + 1)
                nc.gpsimd.tensor_tensor(rest[:, of], rot[u][:, of], parts[u][:, 0, of],
                                        ALU.subtract).then_inc(rest_ready, 1)

            def last_part(n, u, q):
                of = slice(KD * q, KD * (q + 1))
                pool.wait_ge(part1_ready, n * 2 + q + 1)
                nc.gpsimd.tensor_tensor(parts[u][:, 2, of], rest[:, of], parts[u][:, 1, of],
                                        ALU.subtract).then_inc(part2_ready, 1)

            def beginning(n, u):
                rests(n, u, 0)
                pool.wait_ge(halves_ready, n + 2)
                nc.gpsimd.tensor_tensor(rot[u][:, KD:], cosed[1][:], swapped[1][:], ALU.add).then_inc(rot_ready[1], 1)
                last_part(n, u, 0)

            beginning(0, 0)

            def body(pool, b, c, ahead):
                n, u = b * NC + c, c % 2
                rests(n, u, 1)
                last_part(n, u, 1)
                if ahead >= 1:
                    beginning(n + 1, 1 - u)

            over_chunks(body)(pool)

        @block.vector
        def _(dve):
            dve.sem_inc(rot_ready[0], 1)
            dve.sem_inc(halves_ready, 1)
            for q in range(2):
                dve.sem_inc(qk_read[q], 1)
            dve.sem_inc(xnT_ready, LEAD)

            def statistics(n, loads, u):
                dve.wait_ge(x_loaded[u], 16 * loads)
                for t in range(TT):
                    ins = nc.vector.bn_stats(stats[:, t], x_sb[u][:, t])
                ins.then_inc(ln_step, 1)
                wait_alone(dve, ln_step, n * LN_STEPS + 1, passed)
                for t in range(TT):
                    ins = nc.vector.bn_aggr(mv[:, t], stats[:, t])
                ins.then_inc(var_ready, 1)

            def factors(n):
                dve.wait_ge(std_ready, n + 1)
                dve.wait_ge(xn_ready, done(n) - 1)
                nc.vector.reciprocal(rstd[:], std[:]).then_inc(ln_step, 1)
                dve.wait_ge(ln_step, n * LN_STEPS + 2)
                nc.vector.scalar_tensor_tensor(out=shift[:], in0=mv[:, :, 0:1], scalar=-1.0, in1=rstd[:],
                                               op0=ALU.mult, op1=ALU.mult).then_inc(shift_ready, 1)

            def lows(n, u):
                dve.wait_ge(xnT_high_ready, n + 1)
                nc.vector.tensor_tensor(xnT[u][1][:], bank[:, 0:KD, :], xnT[u][0][:].bitcast(F32),
                                        ALU.subtract).then_inc(xnT_ready, 1)

            def rotate(n, u, c, q):
                def table(of_angles):
                    return of_angles[:, c * CH:(c + 1) * CH].unsqueeze(1).to_broadcast([P, KD, CH])

                wait_alone(dve, qk_summed, n * 2 + q + 1, passed)
                nc.vector.stream_shuffle(swapped[q][:], bank[:, 2 + KD * q:2 + KD * (q + 1), :],
                                         [i ^ 1 for i in range(32)]).then_inc(rope_step, 1)
                nc.vector.tensor_tensor(cosed[q][:], bank[:, 2 + KD * q:2 + KD * (q + 1), :], table(cos_sb),
                                        ALU.mult).then_inc(qk_read[q], 1)
                dve.wait_ge(rope_step, n * ROPE_STEPS + q + 1)
                ins = nc.vector.tensor_tensor(swapped[q][:], swapped[q][:], table(sin_sb), ALU.mult)
                if q == 1:
                    ins.then_inc(halves_ready, 1)
                    return
                ins.then_inc(q_step, 1)
                dve.wait_ge(q_step, n + 1)
                nc.vector.tensor_tensor(rot[u][:, 0:KD], cosed[0][:], swapped[0][:], ALU.add).then_inc(rot_ready[0], 1)

            statistics(0, 1, 0)
            factors(0)
            dve.wait_ge(w_high_ready, 1)
            nc.vector.tensor_tensor(w[1][:], w_in[:], w[0][:].bitcast(F32), ALU.subtract).then_inc(w_ready, 1)
            statistics(1, 1, 1)
            factors(1)
            lows(0, 0)
            dve.wait_ge(gram_summed, 1)
            dve.wait_ge(head_loaded, 16)
            nc.vector.tensor_tensor(gram[:], bank[:, 2:2 + NT, 0:P], head_sb[:].unsqueeze(1).to_broadcast([P, NT, P]),
                                    ALU.mult).then_inc(gram_step, 1)
            nc.vector.tensor_reduce(limits[:, 2:3], w_in[:].rearrange("p k n -> p (k n)"), AX.X, ALU.max,
                                    apply_absolute_value=True).then_inc(gram_step, 1)
            dve.wait_ge(gram_step, 1)
            nc.vector.tensor_reduce(row_sums[:], gram[:], AX.X, ALU.add, apply_absolute_value=True).then_inc(gram_step, 1)
            dve.wait_ge(gram_step, 3)
            nc.vector.tensor_reduce(limits[:, 0:2], row_sums[:].rearrange("p (q k) -> p q k", q=2), AX.X, ALU.max)\
              .then_inc(gram_step, 1)

            def body(dve, b, c, ahead):
                n, u = b * NC + c, c % 2
                if ahead >= 2:
                    statistics(n + 2, halves(b, c) + 1, u)
                dve.wait_ge(part2_ready, two_before(n) * 2)
                rotate(n, u, c, 0)
                if ahead >= 1:
                    lows(n + 1, 1 - u)
                if ahead >= 2:
                    factors(n + 2)
                dve.wait_ge(rot_ready[1], n + 1)
                rotate(n, u, c, 1)

            over_chunks(body)(dve)
            dve.wait_ge(limits_turned, 1)
            nc.vector.tensor_reduce(largest[:], bank[0:1, 0, 0:3 * P].rearrange("p (j r) -> p j r", j=3), AX.X, ALU.max)\
              .then_inc(gram_step, 1)
            dve.wait_ge(gram_step, 5)
            nc.vector.tensor_tensor(within[:, 0:1], largest[:, 0:1], largest[:, 1:2], ALU.mult)
            nc.vector.tensor_scalar(within[:, 1:2], largest[:, 2:3], WEIGHT_BOUND, None, ALU.is_le).then_inc(gram_step, 1)
            dve.wait_ge(gram_step, 6)
            nc.vector.tensor_scalar(largest[:, 0:1], within[:, 0:1], (SCORE_BOUND * HD / D) ** 2, None, ALU.is_le)\
              .then_inc(gram_step, 1)
            dve.wait_ge(gram_step, 7)
            nc.vector.tensor_tensor(bounded[:], largest[:, 0:1], within[:, 1:2], ALU.mult).then_inc(gram_step, 1)
            dve.wait_ge(gram_step, 8)


def attend(nc, ctx, tri, bounded, bank, parts_dram, v_dram, att_dram):
    def sb(name, shape, dt=F32):
        return ctx.enter_context(nc.sbuf_tensor(name, shape, dt))

    def sem(name):
        return ctx.enter_context(nc.semaphore(name))

    q_sb = [sb(f"b_q{u}", [R * HD, JH, N], BF16) for u in range(2)]
    k_sb = [sb(f"b_k{u}", [R * HD, JH, N], BF16) for u in range(2)]
    v_sb = [sb(f"b_v{u}", [P, NKB, JH, 2 * HD]) for u in range(2)]
    tri_sb = sb("b_tri", [P, 2, P])
    PB = 8
    probs = [sb(f"b_probs{i}", [P, 2, CH]) for i in range(PB)]
    o_sb = [sb(f"b_o{i}", [P, CH]) for i in range(2)]
    sums = sb("b_sums", [P, CH])
    o_norm = [sb(f"b_on{i}", [P, CH]) for i in range(2)]

    passed = sem("b_passed")
    tri_loaded = sem("b_tri_loaded")
    qkv_loaded = [sem(f"b_qkv_loaded{u}") for u in range(2)]
    scores_summed = sem("b_scores_summed")
    probs_ready = sem("b_probs_ready")
    probs_masked = sem("b_probs_masked")
    steps_summed = sem("b_steps_summed")
    o_copied = sem("b_o_copied")
    norm_step = sem("b_norm_step")
    o_ready = sem("b_o_ready")
    o_stored = [sem(f"b_o_stored{i}") for i in range(2)]

    LOADS = 2 * R + 1
    steps = [(c, kb) for c in range(NC) for kb in range((c + 1) * TT)]
    GS = len(steps)
    body_steps = [(u, c, kb) for u in range(2) for c, kb in steps]
    SB = len(body_steps)
    on_diagonal = [kb >= c * TT for _, c, kb in body_steps]
    MB = 2 * sum(on_diagonal)
    last_of_chunk = [kb == (c + 1) * TT - 1 for _, c, kb in body_steps]

    def slot(m):
        return bank[:, 2 * (m % 3):2 * (m % 3) + 2, :]

    def first_column(c, kb):
        return max(0, kb - c * TT) * P

    with nc.Block() as block:
        @block.sync
        def _(sp):
            with where(sp, bounded, 1):
                def load(b, g, u):
                    for to, picked, q in ((q_sb, QPART, 0), (k_sb, KPART, 1)):
                        for r, part in enumerate(picked):
                            sp.dma_start(to[u][r * HD:(r + 1) * HD, :, :],
                                         parts_dram[part, q, bass.ds(b, 1), g * JH * HD:(g + 1) * JH * HD, :]
                                         .rearrange("o (j d) t -> d (o j) t", d=HD)).then_inc(qkv_loaded[u], 16)
                    sp.dma_start(v_sb[u][:].rearrange("p k j r -> p (k j r)"),
                                 v_dram[bass.ds(b, 1), :, g].rearrange("o p k r -> (o p) (k r)")).then_inc(qkv_loaded[u], 16)

                def stores(b, g):
                    for c in range(NC):
                        k = c % 2
                        wait_alone(sp, o_ready, done(b * NG * NC + g * NC + c), passed)
                        for j in range(JH):
                            row = (g * JH + j) * HD
                            sp.dma_start(att_dram[bass.ds(b * NC + c, 1), row:row + HD, :].rearrange("o d t -> (o d) t"),
                                         o_norm[k][j * 2 * HD:j * 2 * HD + HD, :]).then_inc(o_stored[k], 16)

                sp.dma_start(tri_sb[:], tri).then_inc(tri_loaded, 16)
                for u in range(2):
                    sp.sem_inc(o_stored[u], 16 * JH)
                    load(0, u, u)

                def sequence(b, last):
                    for g in range(NG):
                        stores(b, g)
                        if g + 2 < NG or not last:
                            wait_alone(sp, steps_summed, (b * NG + g + 1) * GS, passed)
                            load(b + (g + 2) // NG, (g + 2) % NG, g % 2)

                with sp.Fori(0, B - 1) as b:
                    sequence(b, False)
                sequence(B - 1, True)
                for k in range(2):
                    sp.wait_ge(o_stored[k], 16 * JH * (B * NG * NC // 2 + 1))

        @block.tensor
        def _(pe):
            with where(pe, bounded, 1):
                with pe.Fori(0, B * NG // 2) as i:
                    def scores(m):
                        u, c, kb = body_steps[m // 2]
                        if m % (2 * GS) == 0:
                            pe.wait_ge(qkv_loaded[u], 16 * LOADS * (i + 1))
                        if m >= 3:
                            pe.wait_ge(probs_ready, i * 2 * SB + m - 2)
                        off = first_column(c, kb)
                        for h in range(2):
                            j = 2 * (m % 2) + h
                            mm = pe.matmul(slot(m)[:, h, off:CH], k_sb[u][:, j, kb * P:(kb + 1) * P],
                                           q_sb[u][:, j, c * CH + off:(c + 1) * CH], start=True, stop=True)
                        mm.then_inc(scores_summed, 1)

                    def outputs(n):
                        u, c, kb = body_steps[n]
                        if on_diagonal[n]:
                            pe.wait_ge(probs_masked, i * MB + 2 * sum(on_diagonal[:n + 1]))
                        else:
                            pe.wait_ge(probs_ready, i * 2 * SB + 2 * n + 2)
                        if kb == 0:
                            pe.wait_ge(o_copied, two_before(i * 2 * NC + u * NC + c))
                        off = first_column(c, kb)
                        for j in range(JH):
                            mm = pe.matmul(bank[2 * HD * j:2 * HD * (j + 1), 6 + c % 2, off:CH], v_sb[u][:, kb, j, :],
                                           probs[(2 * n + j // 2) % PB][:, j % 2, off:CH],
                                           start=(kb == 0), stop=last_of_chunk[n])
                        mm.then_inc(steps_summed, 1)

                    scores(0)
                    scores(1)
                    scores(2)
                    for n in range(SB):
                        if n + 1 < SB:
                            scores(2 * n + 3)
                        if n >= 1:
                            outputs(n - 1)
                        if n + 2 < SB:
                            scores(2 * n + 4)
                    outputs(SB - 1)

        @block.scalar
        def _(act):
            with where(act, bounded, 1):
                with act.Fori(0, B * NG // 2) as i:
                    for m in range(2 * SB):
                        u, c, kb = body_steps[m // 2]
                        act.wait_ge(scores_summed, i * 2 * SB + m + 1)
                        if m >= PB:
                            act.wait_ge(steps_summed, i * SB + (m - PB) // 2 + 1)
                        off = first_column(c, kb)
                        nc.scalar.activation(probs[m % PB][:, :, off:CH], slot(m)[:, :, off:CH], ACT.Exp,
                                             scale=1.0 / HD).then_inc(probs_ready, 1)

        @block.gpsimd
        def _(pool):
            with where(pool, bounded, 1):
                pool.wait_ge(tri_loaded, 16)
                with pool.Fori(0, B * NG // 2) as i:
                    for m in range(2 * SB):
                        u, c, kb = body_steps[m // 2]
                        if on_diagonal[m // 2]:
                            off = first_column(c, kb)
                            pool.wait_ge(probs_ready, i * 2 * SB + m + 1)
                            nc.gpsimd.tensor_tensor(probs[m % PB][:, :, off:off + P], probs[m % PB][:, :, off:off + P],
                                                    tri_sb[:], ALU.mult).then_inc(probs_masked, 1)

        @block.vector
        def _(dve):
            with where(dve, bounded, 1):
                dve.sem_inc(o_copied, LEAD)
                dve.sem_inc(o_ready, LEAD)
                with dve.Fori(0, B * NG // 2) as i:
                    for n in range(SB):
                        if not last_of_chunk[n]:
                            continue
                        u, c, _ = body_steps[n]
                        k, q = c % 2, u * NC + c
                        dve.wait_ge(steps_summed, i * SB + n + 1)
                        nc.vector.tensor_copy(o_sb[k][:], bank[:, 6 + k, :]).then_inc(o_copied, 1)
                        wait_alone(dve, o_copied, done(i * 2 * NC + q), passed)
                        nc.vector.stream_shuffle(sums[:], o_sb[k][:], [HD + r % HD for r in range(2 * HD)])\
                          .then_inc(norm_step, 1)
                        dve.wait_ge(norm_step, i * 4 * NC + 2 * q + 1)
                        nc.vector.reciprocal(sums[:], sums[:]).then_inc(norm_step, 1)
                        dve.wait_ge(norm_step, i * 4 * NC + 2 * q + 2)
                        dve.wait_ge(o_stored[k], 16 * JH * (i * NC + q // 2 + 1))
                        nc.vector.tensor_tensor(o_norm[k][:], o_sb[k][:], sums[:], ALU.mult).then_inc(o_ready, 1)


def attend_unbounded(nc, ctx, causal, bounded, ident_sb, bank, parts_dram, v_dram, att_dram):
    def sb(name, shape, dt=F32):
        return ctx.enter_context(nc.sbuf_tensor(name, shape, dt))

    def sem(name):
        return ctx.enter_context(nc.semaphore(name))

    q_sb = sb("g_q", [R * HD, JH, N], BF16)
    k_sb = sb("g_k", [R * HD, JH, N], BF16)
    v_sb = sb("g_v", [P, NKB, JH, 2 * HD])
    causal_sb = sb("g_causal", [P, 2 * N - P])
    scores = sb("g_scores", [P, N])
    top = sb("g_top", [P, 1])
    minus_top = sb("g_minus_top", [P, 1])
    probs = sb("g_probs", [P, N])
    probsT = sb("g_probsT", [P, N])
    o_sb = sb("g_o", [2 * HD, P])
    sums = sb("g_sums", [2 * HD, P])
    o_norm = sb("g_on", [2 * HD, P])

    passed = sem("g_passed")
    causal_loaded = sem("g_causal_loaded")
    qkv_loaded = sem("g_qkv_loaded")
    scores_summed = sem("g_scores_summed")
    scores_masked = sem("g_scores_masked")
    top_found = sem("g_top_found")
    top_negated = sem("g_top_negated")
    probs_ready = sem("g_probs_ready")
    probs_turned = sem("g_probs_turned")
    probsT_ready = sem("g_probsT_ready")
    o_summed = sem("g_o_summed")
    o_copied = sem("g_o_copied")
    sums_beside = sem("g_sums_beside")
    inverted = sem("g_inverted")
    o_ready = sem("g_o_ready")
    o_stored = sem("g_o_stored")

    LOADS = 2 * R + 1
    GT = JH * NKB

    def over_tiles(eng, group, tile):
        with eng.Fori(0, B) as b:
            with eng.Fori(0, NG) as g:
                i = b * NG + g
                group(b, g, i)
                for j in range(JH):
                    with eng.Fori(0, NC) as c:
                        for s in range(TT):
                            tile(b, g, j, c, s, i * GT + j * NKB + c * TT + s)

    def none(b, g, i):
        pass

    with nc.Block() as block:
        @block.sync
        def _(sp):
            with where(sp, bounded, 0):
                sp.dma_start(causal_sb[:], causal).then_inc(causal_loaded, 16)
                sp.sem_inc(o_stored, 16)

                def load(b, g, i):
                    wait_alone(sp, o_stored, 16 * (i * GT + 1), passed)
                    for to, picked, q in ((q_sb, QPART, 0), (k_sb, KPART, 1)):
                        for r, part in enumerate(picked):
                            sp.dma_start(to[r * HD:(r + 1) * HD, :, :],
                                         parts_dram[part, q, bass.ds(b, 1), bass.ds(g * JH * HD, JH * HD), :]
                                         .rearrange("o (j d) t -> d (o j) t", d=HD)).then_inc(qkv_loaded, 16)
                    sp.dma_start(v_sb[:].rearrange("p k j r -> p (k j r)"),
                                 v_dram[bass.ds(b, 1), :, bass.ds(g, 1)].rearrange("o p e k r -> (o p e) (k r)"))\
                      .then_inc(qkv_loaded, 16)

                def store(b, g, j, c, s, n):
                    wait_alone(sp, o_ready, n + 1, passed)
                    sp.dma_start(att_dram[bass.ds(b * NC + c, 1), bass.ds(g * JH * HD + j * HD, HD), s * P:(s + 1) * P]
                                 .rearrange("o d t -> (o d) t"), o_norm[0:HD, :]).then_inc(o_stored, 16)

                over_tiles(sp, load, store)
                sp.wait_ge(o_stored, 16 * (B * NG * GT + 1))

        @block.tensor
        def _(pe):
            with where(pe, bounded, 0):
                def loaded(b, g, i):
                    wait_alone(pe, qkv_loaded, 16 * LOADS * (i + 1), passed)

                def tile(b, g, j, c, s, n):
                    for k in range(NC):
                        mm = pe.matmul(bank[:, k, :], q_sb[:, j, bass.ds(c * CH + s * P, P)],
                                       k_sb[:, j, k * CH:(k + 1) * CH], start=True, stop=True)
                    mm.then_inc(scores_summed, 1)
                    pe.wait_ge(probs_ready, n + 1)
                    for k in range(NKB):
                        mm = pe.transpose(bank[:, k // TT, k % TT * P:(k % TT + 1) * P], probs[:, k * P:(k + 1) * P],
                                          ident_sb[:])
                    mm.then_inc(probs_turned, 1)
                    pe.wait_ge(probsT_ready, n + 1)
                    for k in range(NKB):
                        mm = pe.matmul(bank[0:2 * HD, 4, 0:P], v_sb[:, k, j, :], probsT[:, k * P:(k + 1) * P],
                                       start=(k == 0), stop=(k == NKB - 1))
                    mm.then_inc(o_summed, 1)

                over_tiles(pe, loaded, tile)

        @block.scalar
        def _(act):
            with where(act, bounded, 0):
                def tile(b, g, j, c, s, n):
                    act.wait_ge(top_negated, n + 1)
                    nc.scalar.activation(probs[:], scores[:], ACT.Exp, bias=minus_top[:, 0:1]).then_inc(probs_ready, 1)
                    act.wait_ge(probs_turned, n + 1)
                    nc.scalar.copy(probsT[:].rearrange("p (k t) -> p k t", k=NC), bank[:, 0:NC, :])\
                      .then_inc(probsT_ready, 1)

                over_tiles(act, none, tile)

        @block.vector
        def _(dve):
            with where(dve, bounded, 0):
                dve.wait_ge(causal_loaded, 16)

                def tile(b, g, j, c, s, n):
                    wait_alone(dve, scores_summed, n + 1, passed)
                    nc.vector.scalar_tensor_tensor(
                        out=scores[:].rearrange("p (k t) -> p k t", k=NC), in0=bank[:, 0:NC, :], scalar=1.0 / HD,
                        in1=causal_sb[:, bass.ds(N - P - s * P - c * CH, N)].rearrange("p (k t) -> p k t", k=NC),
                        op0=ALU.mult, op1=ALU.add).then_inc(scores_masked, 1)
                    dve.wait_ge(scores_masked, n + 1)
                    nc.vector.tensor_reduce(top[:], scores[:], AX.X, ALU.max).then_inc(top_found, 1)
                    dve.wait_ge(top_found, n + 1)
                    nc.vector.tensor_scalar(minus_top[:], top[:], -1.0, None, ALU.mult).then_inc(top_negated, 1)
                    dve.wait_ge(o_summed, n + 1)
                    nc.vector.tensor_copy(o_sb[:], bank[0:2 * HD, 4, 0:P]).then_inc(o_copied, 1)
                    wait_alone(dve, o_copied, n + 1, passed)
                    nc.vector.stream_shuffle(sums[:], o_sb[:], [HD + r % HD for r in range(2 * HD)])\
                      .then_inc(sums_beside, 1)
                    dve.wait_ge(sums_beside, n + 1)
                    nc.vector.reciprocal(sums[:], sums[:]).then_inc(inverted, 1)
                    dve.wait_ge(inverted, n + 1)
                    dve.wait_ge(o_stored, 16 * (n + 1))
                    nc.vector.tensor_tensor(o_norm[:], o_sb[:], sums[:], ALU.mult).then_inc(o_ready, 1)

                over_tiles(dve, none, tile)


def experts(nc, ctx, x, wo, bo, w1, b1, w2, b2, cent, wr, ident_sb, bank, att_dram, out):
    def sb(name, shape, dt=F32):
        return ctx.enter_context(nc.sbuf_tensor(name, shape, dt))

    def sem(name):
        return ctx.enter_context(nc.semaphore(name))

    wo_in = sb("c_wo_in", [P, KD, D])
    w1_in = sb("c_w1_in", [P, KD, E, F])
    w2_in = sb("c_w2_in", [P, E, D])
    wo_sb = [sb(f"c_wo{i}", [P, KD, D], F32R) for i in range(2)]
    bo_sb = sb("c_bo", [P, TT, D])
    w1_sb = [sb(f"c_w1{i}", [P, KD, E, F], F32R) for i in range(2)]
    b1_sb = sb("c_b1", [P, E])
    w2_sb = [sb(f"c_w2{i}", [P, E, D], F32R) for i in range(2)]
    b2_sb = sb("c_b2", [E, D])
    cent_sb = sb("c_cent", [E, D])
    cent_sq = sb("c_cent_sq", [E, D])
    cent_n = sb("c_cent_n", [E, 1])
    cent_s = sb("c_cent_s", [E, 1])
    wr_sb = sb("c_wr", [E, D])
    route = sb("c_route", [P, KD, 32])
    minus_half = sb("c_minus_half", [P, TT])
    half = sb("c_half", [P, TT])
    att_sb = [sb(f"c_att{u}", [P, KD, CH]) for u in range(2)]
    att = [[sb(f"c_att{u}{i}", [P, KD, CH], F32R) for i in range(2)] for u in range(2)]
    x_sb = [sb(f"c_x{u}", [P, TT, D]) for u in range(2)]
    x2 = [sb(f"c_x2{u}", [P, TT, D]) for u in range(2)]
    xn = [sb(f"c_xn{u}", [P, TT, D]) for u in range(2)]
    xnT32 = [sb(f"c_xnT32{u}", [P, KD, CH]) for u in range(2)]
    xnT = [[sb(f"c_xnT{u}{i}", [P, KD, CH], F32R) for i in range(2)] for u in range(2)]
    scoresT = sb("c_scoresT", [P, P])
    stats = sb("c_stats", [P, TT, 6])
    mv = sb("c_mv", [P, TT, 2])
    var_eps = sb("c_var_eps", [P, TT])
    rstd = sb("c_rstd", [P, TT])
    sq = sb("c_sq", [P, TT])
    root = sb("c_root", [P, TT])
    length = [sb(f"c_length{u}", [P, TT]) for u in range(2)]
    scored = sb("c_scored", [P, TT, 2 * E])
    logits = sb("c_logits", [P, TT, E])
    top = sb("c_top", [P, TT, 8])
    shifted = sb("c_shifted", [P, TT, E])
    kept = sb("c_kept", [P, TT, E])
    exps = sb("c_exps", [P, TT, E])
    total = sb("c_total", [P, TT])
    gates = [sb(f"c_gates{u}", [P, TT, E]) for u in range(2)]
    gatesT = sb("c_gatesT", [E, CH])
    HB = 4
    hid32 = [sb(f"c_hid32{i}", [P, CH]) for i in range(HB)]
    hid = [sb(f"c_hid{i}", [P, E, CH], F32R) for i in range(2)]
    acc = [sb(f"c_acc{u}", [P, TT, D]) for u in range(2)]
    y = [sb(f"c_y{u}", [P, TT, D]) for u in range(2)]

    passed = sem("c_passed")
    weights_loaded = sem("c_weights_loaded")
    att_loaded = [sem(f"c_att_loaded{u}") for u in range(2)]
    out_stored = [sem(f"c_out_stored{u}") for u in range(2)]
    consts_set = sem("c_consts_set")
    cent_step = sem("c_cent_step")
    cent_rooted = sem("c_cent_rooted")
    routeT_summed = sem("c_routeT_summed")
    route_ready = sem("c_route_ready")
    o_summed = sem("c_o_summed")
    x_added = sem("c_x_added")
    x2_ready = sem("c_x2_ready")
    ln_step = sem("c_ln_step")
    var_ready = sem("c_var_ready")
    rstd_ready = sem("c_rstd_ready")
    xn_ready = sem("c_xn_ready")
    xnT_summed = sem("c_xnT_summed")
    xnT_high_ready = sem("c_xnT_high_ready")
    xnT_ready = sem("c_xnT_ready")
    weights_high = sem("c_weights_high")
    weights_ready = sem("c_weights_ready")
    att_high = sem("c_att_high")
    att_ready = sem("c_att_ready")
    scoresT_summed = sem("c_scoresT_summed")
    scoresT_ready = sem("c_scoresT_ready")
    hid32_ready = sem("c_hid32_ready")
    hid_high = sem("c_hid_high")
    scores_summed = sem("c_scores_summed")
    gate_step = sem("c_gate_step")
    exps_ready = sem("c_exps_ready")
    gates_ready = sem("c_gates_ready")
    gatesT_summed = sem("c_gatesT_summed")
    gatesT_ready = sem("c_gatesT_ready")
    hid_summed = sem("c_hid_summed")
    hid_ready = sem("c_hid_ready")
    y_summed = sem("c_y_summed")
    y_added = sem("c_y_added")

    YB = (E + 1) * TT // 2
    LN_STEPS = 2
    GATE_STAGES = 10
    WEIGHTS = 8 + TT

    with nc.Block() as block:
        def over_chunks(body, apart=1):
            def run(eng):
                with eng.Fori(0, NCH // 2 - apart) as i:
                    for u in range(2):
                        body(eng, i, u, 2 * i + u, 2 * apart)
                for n in range(NCH - 2 * apart, NCH):
                    body(eng, n // 2, n % 2, n, NCH - 1 - n)
            return run

        @block.sync
        def _(sp):
            def load(n, u):
                sp.dma_start(att_sb[u][:], att_dram[bass.ds(n, 1)].rearrange("o (k p) t -> p (o k) t", p=P))\
                  .then_inc(att_loaded[u], 16)
                sp.dma_start(x_sb[u][:], x[bass.ds(n * CH, CH), :].rearrange("(t p) d -> p t d", p=P))\
                  .then_inc(att_loaded[u], 16)

            weights = [(cent_sb[:], cent), (wr_sb[:], wr), (wo_in[:], wo.rearrange("(k p) n -> p k n", p=P)),
                       (w1_in[:, 0], w1[:, 0:P, :].rearrange("e p f -> p e f")),
                       (w1_in[:, 1], w1[:, P:D, :].rearrange("e p f -> p e f")), (b1_sb[:], b1),
                       (w2_in[:], w2.rearrange("e f d -> f e d")), (b2_sb[:], b2)]
            weights += [(bo_sb[:, t], bo.partition_broadcast(P)) for t in range(TT)]
            load(0, 0)
            for k, (to, source) in enumerate(weights):
                sp.dma_start(to, source).then_inc(weights_loaded, 16)
            load(1, 1)
            sp.wait_ge(att_ready, 1)
            sp.wait_ge(x_added, 1)
            load(2, 0)

            def body(sp, i, u, n, ahead):
                if ahead >= 3:
                    sp.wait_ge(att_ready, n + 2)
                    wait_alone(sp, x_added, n + 2, passed)
                    load(n + 3, 1 - u)
                wait_alone(sp, y_added, done(n) * YB, passed)
                sp.dma_start(out[bass.ds(n * CH, CH), :].rearrange("(t p) d -> p t d", p=P), y[u][:])\
                  .then_inc(out_stored[u], 16)

            over_chunks(body, apart=2)(sp)
            for u in range(2):
                sp.wait_ge(out_stored[u], 16 * (NCH // 2 + 1))

        @block.tensor
        def _(pe):
            def projected(n, u):
                pe.wait_ge(att_ready, n + 1)
                for t in range(TT):
                    for k in range(KD):
                        for i, (a, z) in enumerate(PRODUCTS):
                            mm = pe.matmul(bank[:, 2 + t // 2, (t % 2) * D:(t % 2 + 1) * D],
                                           att[u][a][:, k, t * P:(t + 1) * P], wo_sb[z][:, k, :],
                                           start=(k + i == 0), stop=(k == KD - 1 and i == 2))
                mm.then_inc(o_summed, 1)

            def turned(n, u):
                pe.wait_ge(xn_ready, done(n))
                pe.wait_ge(xnT_ready, done(n) - 1)
                for k in range(KD):
                    for t in range(TT):
                        mm = pe.transpose(bank[:, 4 + k, t * P:(t + 1) * P], xn[u][:, t, k * P:(k + 1) * P], ident_sb[:])
                mm.then_inc(xnT_summed, 1)

            def routed(n, u):
                pe.wait_ge(xnT_ready, done(n))
                for k in range(KD):
                    for t in range(TT):
                        mm = pe.matmul(bank[32 * t:32 * (t + 1), 2, 0:P], route[:, k, :],
                                       xnT32[u][:, k, t * P:(t + 1) * P], start=(k == 0), stop=(k == KD - 1))
                mm.then_inc(scoresT_summed, 1)

            def scored_back(n):
                pe.wait_ge(scoresT_ready, n + 1)
                pe.transpose(bank[:, 2, P:2 * P], scoresT[:], ident_sb[:]).then_inc(scores_summed, 1)

            def first_product(n, u, e):
                pe.wait_ge(xnT_ready, done(n))
                pe.wait_ge(hid32_ready, n * E + e - 1 + LEAD * E)
                for k in range(KD):
                    for i, (a, z) in enumerate(PRODUCTS):
                        mm = pe.matmul(bank[:, e % 2, :], w1_sb[a][:, k, e, :], xnT[u][z][:, k, :],
                                       start=(k + i == 0), stop=(k == KD - 1 and i == 2))
                mm.then_inc(hid_summed, 1)

            def second_product(n, e):
                pe.wait_ge(hid_ready, n * E + e + 1)
                for t in range(TT):
                    m = e * TT // 2 + t // 2
                    if t % 2 == 0:
                        pe.wait_ge(y_added, n * YB + m - 1 + LEAD * YB)
                    for i, (a, z) in enumerate(PRODUCTS):
                        mm = pe.matmul(bank[:, 6 + m % 2, (t % 2) * D:(t % 2 + 1) * D],
                                       hid[a][:, e, t * P:(t + 1) * P], w2_sb[z][:, e, :],
                                       start=(i == 0), stop=(i == 2))
                    if t % 2 == 1:
                        mm.then_inc(y_summed, 1)

            def turned_gates(n, u):
                pe.wait_ge(gates_ready, n + 1)
                for t in range(TT):
                    mm = pe.transpose(bank[0:E, 3, t * P:(t + 1) * P], gates[u][:, t, :], ident_sb[:])
                mm.then_inc(gatesT_summed, 1)

            def last_bias(n):
                pe.wait_ge(gatesT_ready, n + 1)
                for t in range(TT):
                    m = E * TT // 2 + t // 2
                    if t % 2 == 0:
                        pe.wait_ge(y_added, n * YB + m - 1 + LEAD * YB)
                    mm = pe.matmul(bank[:, 6 + m % 2, (t % 2) * D:(t % 2 + 1) * D],
                                   gatesT[:, t * P:(t + 1) * P], b2_sb[:], start=True, stop=True)
                    if t % 2 == 1:
                        mm.then_inc(y_summed, 1)

            pe.sem_inc(xnT_summed, LEAD)
            pe.wait_ge(weights_loaded, 16 * WEIGHTS)
            pe.wait_ge(weights_ready, 1)
            projected(0, 0)
            pe.wait_ge(cent_step, 4)
            for k in range(KD):
                pe.transpose(bank[:, 4, k * 2 * E:k * 2 * E + E], cent_sb[:, k * P:(k + 1) * P], ident_sb[0:E, 0:E])
                mm = pe.transpose(bank[:, 4, k * 2 * E + E:(k + 1) * 2 * E], wr_sb[:, k * P:(k + 1) * P], ident_sb[0:E, 0:E])
            mm.then_inc(routeT_summed, 1)
            pe.wait_ge(route_ready, 2)
            turned(0, 0)
            pe.wait_ge(x2_ready, 1)
            projected(1, 1)
            pe.wait_ge(weights_ready, 2)
            for e in range(E):
                first_product(0, 0, e)
            turned(1, 1)
            routed(0, 0)
            scored_back(0)
            pe.wait_ge(weights_ready, 3)

            def body(pe, i, u, n, ahead):
                for e in range(E):
                    second_product(n, e)
                    if ahead >= 1:
                        first_product(n + 1, 1 - u, e)
                    if e == 0:
                        turned_gates(n, u)
                        if ahead >= 1:
                            routed(n + 1, 1 - u)
                    if e == 1 and ahead >= 1:
                        scored_back(n + 1)
                    if e == 3 and ahead >= 2:
                        pe.wait_ge(gate_step, (n + 1) * GATE_STAGES + 3)
                        pe.wait_ge(gatesT_ready, n + 1)
                        projected(n + 2, u)
                if ahead >= 2:
                    turned(n + 2, u)
                last_bias(n)

            over_chunks(body)(pe)

        @block.scalar
        def _(act):
            act.sem_inc(hid32_ready, LEAD * E)

            def att_highs(n, i, u):
                act.wait_ge(att_loaded[u], 32 * (i + 1))
                act.wait_ge(o_summed, n - 1) if not isinstance(n, int) or n >= 2 else None
                nc.scalar.copy(att[u][0][:], att_sb[u][:]).then_inc(att_high, 1)

            def turned(n, u):
                act.wait_ge(xnT_summed, done(n))
                nc.scalar.copy(xnT[u][0][:], bank[:, 4:4 + KD, :]).then_inc(xnT_high_ready, 1)
                nc.scalar.copy(xnT32[u][:], bank[:, 4:4 + KD, :]).then_inc(xnT_high_ready, 1)

            def scores_out(n):
                act.wait_ge(scoresT_summed, n + 1)
                nc.scalar.copy(scoresT[:], bank[:, 2, 0:P]).then_inc(scoresT_ready, 1)

            def exped(n):
                act.wait_ge(gate_step, n * GATE_STAGES + 6)
                nc.scalar.activation(exps[:], shifted[:], ACT.Exp).then_inc(exps_ready, 1)

            def hidden(n, e):
                act.wait_ge(hid_summed, n * E + e + 1)
                if not isinstance(n, int) or n * E + e >= HB:
                    act.wait_ge(hid_ready, n * E + e + 1 - HB)
                nc.scalar.activation(hid32[e % HB][:], bank[:, e % 2, :], ACT.Gelu, bias=b1_sb[:, e:e + 1])\
                  .then_inc(hid32_ready, 1)
                act.wait_ge(hid32_ready, n * E + e + 1 + LEAD * E)
                nc.scalar.copy(hid[0][:, e, :], hid32[e % HB][:]).then_inc(hid_high, 1)

            act.wait_ge(weights_loaded, 16 * WEIGHTS)
            nc.scalar.copy(wo_sb[0][:], wo_in[:]).then_inc(weights_high, 1)
            att_highs(0, 0, 0)
            nc.scalar.copy(w1_sb[0][:], w1_in[:]).then_inc(weights_high, 1)
            att_highs(1, 0, 1)
            nc.scalar.copy(w2_sb[0][:], w2_in[:]).then_inc(weights_high, 1)
            turned(0, 0)
            for e in range(E):
                hidden(0, e)
            turned(1, 1)
            scores_out(0)
            exped(0)

            def body(act, i, u, n, ahead):
                for e in range(E):
                    if ahead >= 1:
                        hidden(n + 1, e)
                    if e == 0:
                        act.wait_ge(gatesT_summed, n + 1)
                        nc.scalar.copy(gatesT[:], bank[0:E, 3, :]).then_inc(gatesT_ready, 1)
                        if ahead >= 1:
                            scores_out(n + 1)
                        if ahead >= 2:
                            att_highs(n + 2, i + 1, u)
                    if e == 5 and ahead >= 1:
                        exped(n + 1)
                if ahead >= 2:
                    turned(n + 2, u)

            over_chunks(body)(act)

        @block.gpsimd
        def _(pool):
            nc.gpsimd.memset(minus_half[:], -0.5).then_inc(consts_set, 1)
            nc.gpsimd.memset(half[:], 0.5).then_inc(consts_set, 1)
            pool.wait_ge(consts_set, 2)
            pool.wait_ge(cent_step, 2)
            nc.gpsimd.tensor_tensor(cent_s[:], cent_n[:], half[0:E, 0:1], ALU.pow).then_inc(cent_rooted, 1)

            def roots(n):
                pool.wait_ge(var_ready, n + 1)
                nc.gpsimd.tensor_tensor(rstd[:], var_eps[:], minus_half[:], ALU.pow).then_inc(rstd_ready, 1)
                nc.gpsimd.tensor_tensor(root[:], sq[:], half[:], ALU.pow).then_inc(rstd_ready, 1)

            def att_lows(n, u):
                pool.wait_ge(att_high, n + 1)
                nc.gpsimd.tensor_tensor(att[u][1][:], att_sb[u][:], att[u][0][:].bitcast(F32),
                                        ALU.subtract).then_inc(att_ready, 1)

            def x_and_bias(n, i, u):
                pool.wait_ge(att_loaded[u], 32 * (i + 1))
                if not isinstance(n, int) or n >= 2:
                    pool.wait_ge(y_added, (n - 2) * YB + 2 + LEAD * YB)
                nc.gpsimd.tensor_tensor(x2[u][:], x_sb[u][:], bo_sb[:], ALU.add).then_inc(x_added, 1)

            def low(n, e):
                pool.wait_ge(hid_high, n * E + e + 1)
                nc.gpsimd.tensor_tensor(hid[1][:, e, :], hid32[e % HB][:], hid[0][:, e, :].bitcast(F32),
                                        ALU.subtract).then_inc(hid_ready, 1)

            pool.wait_ge(weights_loaded, 16 * WEIGHTS)
            att_lows(0, 0)
            x_and_bias(0, 0, 0)
            att_lows(1, 1)
            roots(0)
            x_and_bias(1, 0, 1)
            for e in range(E):
                low(0, e)
                if e == 1:
                    roots(1)

            def body(pool, i, u, n, ahead):
                for e in range(E):
                    if ahead >= 1:
                        low(n + 1, e)
                    if ahead >= 2:
                        if e == 1:
                            att_lows(n + 2, u)
                        if e == 2:
                            x_and_bias(n + 2, i + 1, u)
                        if e == 5:
                            roots(n + 2)

            over_chunks(body)(pool)

        @block.vector
        def _(dve):
            dve.sem_inc(xn_ready, LEAD)
            dve.sem_inc(xnT_ready, LEAD)
            nc.vector.memset(route[:], 0.0).then_inc(route_ready, 1)
            dve.sem_inc(y_added, LEAD * YB)
            for u in range(2):
                dve.sem_inc(out_stored[u], 16)
            dve.wait_ge(weights_loaded, 16 * WEIGHTS)
            nc.vector.tensor_tensor(cent_sq[:], cent_sb[:], cent_sb[:], ALU.mult).then_inc(cent_step, 1)
            dve.wait_ge(cent_step, 1)
            nc.vector.tensor_reduce(cent_n[:], cent_sq[:], AX.X, ALU.add).then_inc(cent_step, 1)
            dve.wait_ge(weights_high, 1)
            nc.vector.tensor_tensor(wo_sb[1][:], wo_in[:], wo_sb[0][:].bitcast(F32), ALU.subtract).then_inc(weights_ready, 1)
            dve.wait_ge(cent_rooted, 1)
            nc.vector.tensor_scalar(cent_s[:], cent_s[:], 1e-12, None, ALU.max).then_inc(cent_rooted, 1)
            dve.wait_ge(cent_rooted, 2)
            nc.vector.reciprocal(cent_n[:], cent_s[:]).then_inc(cent_step, 1)
            dve.wait_ge(cent_step, 3)
            nc.vector.tensor_scalar(cent_sb[:], cent_sb[:], cent_n[:, 0:1], None, ALU.mult).then_inc(cent_step, 1)
            dve.wait_ge(routeT_summed, 1)
            dve.wait_ge(route_ready, 1)
            nc.vector.tensor_copy(route[:, :, 0:2 * E], bank[:, 4, 0:KD * 2 * E].rearrange("p (k e) -> p k e", k=KD))\
              .then_inc(route_ready, 1)

            def lows(n, u):
                dve.wait_ge(xnT_high_ready, 2 * (n + 1))
                nc.vector.tensor_tensor(xnT[u][1][:], bank[:, 4:4 + KD, :], xnT[u][0][:].bitcast(F32),
                                        ALU.subtract).then_inc(xnT_ready, 1)

            def norm(n, u, stage):
                if stage == 0:
                    dve.wait_ge(x_added, n + 1)
                    dve.wait_ge(o_summed, n + 1)
                    nc.vector.tensor_tensor(x2[u][:], bank[:, 2:4, :].rearrange("p a (b d) -> p (a b) d", b=2), x2[u][:],
                                            ALU.add).then_inc(x2_ready, 1)
                if stage == 1:
                    dve.wait_ge(x2_ready, n + 1)
                    for t in range(TT):
                        ins = nc.vector.bn_stats(stats[:, t], x2[u][:, t])
                    ins.then_inc(ln_step, 1)
                if stage == 2:
                    wait_alone(dve, ln_step, n * LN_STEPS + 1, passed)
                    for t in range(TT):
                        ins = nc.vector.bn_aggr(mv[:, t], stats[:, t])
                    ins.then_inc(ln_step, 1)
                    dve.wait_ge(ln_step, n * LN_STEPS + 2)
                    nc.vector.tensor_scalar(sq[:], mv[:, :, 1], float(D), None, ALU.mult)
                    nc.vector.tensor_scalar(var_eps[:], mv[:, :, 1], 1e-5, None, ALU.add).then_inc(var_ready, 1)
                if stage == 3:
                    dve.wait_ge(rstd_ready, 2 * (n + 1))
                    dve.wait_ge(xnT_summed, two_before(n))
                    nc.vector.tensor_tensor(length[u][:], root[:], rstd[:], ALU.mult)
                    for t in range(TT):
                        ins = nc.vector.tensor_scalar(xn[u][:, t], x2[u][:, t], mv[:, t, 0:1], rstd[:, t:t + 1],
                                                      ALU.subtract, ALU.mult)
                    ins.then_inc(xn_ready, 1)

            def gate(n, u, stage):
                def link(ins):
                    ins.then_inc(gate_step, 1)

                if stage == 4:
                    wait_alone(dve, gate_step, n * GATE_STAGES + stage, passed)
                elif stage > 0:
                    dve.wait_ge(gate_step, n * GATE_STAGES + stage)
                if stage == 0:
                    dve.wait_ge(xn_ready, done(n))
                    link(nc.vector.tensor_scalar(length[u][:], length[u][:], 1e-12, None, ALU.max))
                if stage == 1:
                    link(nc.vector.reciprocal(length[u][:], length[u][:]))
                if stage == 2:
                    dve.wait_ge(scores_summed, n + 1)
                    link(nc.vector.tensor_copy(scored[:], bank[:, 2, P:2 * P].rearrange("p (t e) -> p t e", t=TT)[:, :, 0:2 * E]))
                if stage == 3:
                    for t in range(TT):
                        ins = nc.vector.scalar_tensor_tensor(out=logits[:, t], in0=scored[:, t, 0:E],
                                                             scalar=length[u][:, t:t + 1],
                                                             in1=scored[:, t, E:2 * E], op0=ALU.mult, op1=ALU.add)
                    link(ins)
                if stage == 4:
                    for t in range(TT):
                        ins = nc.vector.max(top[:, t], logits[:, t])
                    link(ins)
                if stage == 5:
                    link(nc.vector.tensor_tensor(shifted[:], logits[:], top[:, :, 0:1].to_broadcast([P, TT, E]),
                                                 ALU.subtract))
                if stage == 6:
                    link(nc.vector.tensor_tensor(kept[:], logits[:], top[:, :, 1:2].to_broadcast([P, TT, E]), ALU.is_ge))
                if stage == 7:
                    dve.wait_ge(exps_ready, n + 1)
                    link(nc.vector.tensor_tensor(kept[:], kept[:], exps[:], ALU.mult))
                if stage == 8:
                    link(nc.vector.tensor_reduce(total[:], kept[:], AX.X, ALU.add))
                if stage == 9:
                    link(nc.vector.reciprocal(total[:], total[:]))
                if stage == 10:
                    nc.vector.tensor_tensor(gates[u][:], kept[:], total[:].unsqueeze(2).to_broadcast([P, TT, E]),
                                            ALU.mult).then_inc(gates_ready, 1)

            def add(n, i, u, m):
                e, a = m // 2, m % 2
                dve.wait_ge(y_summed, n * YB + m + 1)
                if m >= 2:
                    dve.wait_ge(y_added, n * YB + m - 1 + LEAD * YB)
                if e < E:
                    for t in (2 * a, 2 * a + 1):
                        ins = nc.vector.scalar_tensor_tensor(
                            out=acc[u][:, t], in0=bank[:, 6 + m % 2, (t % 2) * D:(t % 2 + 1) * D],
                            scalar=gates[u][:, t, e:e + 1], in1=(x2 if e == 0 else acc)[u][:, t],
                            op0=ALU.mult, op1=ALU.add)
                else:
                    if a == 0:
                        dve.wait_ge(out_stored[u], 16 * (i + 1))
                    ins = nc.vector.tensor_tensor(y[u][:, 2 * a:2 * a + 2],
                                                  bank[:, 6 + m % 2, :].rearrange("p (b d) -> p b d", b=2),
                                                  acc[u][:, 2 * a:2 * a + 2], ALU.add)
                ins.then_inc(y_added, 1)

            for stage in range(4):
                norm(0, 0, stage)
            dve.wait_ge(weights_high, 2)
            nc.vector.tensor_tensor(w1_sb[1][:], w1_in[:], w1_sb[0][:].bitcast(F32), ALU.subtract).then_inc(weights_ready, 1)
            lows(0, 0)
            for stage in range(4):
                norm(1, 1, stage)
            dve.wait_ge(weights_high, 3)
            nc.vector.tensor_tensor(w2_sb[1][:], w2_in[:], w2_sb[0][:].bitcast(F32), ALU.subtract).then_inc(weights_ready, 1)
            lows(1, 1)
            for stage in range(GATE_STAGES + 1):
                gate(0, 0, stage)

            def body(dve, i, u, n, ahead):
                dve.wait_ge(gates_ready, n + 1)
                for m in range(YB):
                    add(n, i, u, m)
                    if ahead >= 1 and 0 <= m - 4 <= GATE_STAGES:
                        gate(n + 1, 1 - u, m - 4)
                    if ahead >= 2 and m in (9, 10, 11, 13):
                        norm(n + 2, u, (9, 10, 11, 13).index(m))
                if ahead >= 2:
                    lows(n + 2, u)

            over_chunks(body)(dve)


def kernel(**inputs):
    import numpy as np
    import concourse.bacc as bacc
    from concourse.bass_utils import run_bass_kernel_spmd

    def f(name):
        return np.asarray(inputs[name])

    inv_freq = (np.float32(1.0) / np.power(np.float32(10000.0), np.arange(0, HD, 2, dtype=np.float32) / np.float32(HD)))
    angle = np.arange(N, dtype=np.float32)[:, None] * inv_freq.astype(np.float32)[None, :]
    row = np.arange(P) % HD // 2
    cos = np.cos(angle).astype(np.float32).T[row]
    sin = np.sin(angle).astype(np.float32).T[row] * np.where(np.arange(P) % 2 == 0, -1, 1).astype(np.float32)[:, None]
    tri = (np.arange(P)[None, :] >= np.arange(P)[:, None]).astype(np.float32)
    causal = np.where(np.arange(2 * N - P)[None, :] - (N - P) <= np.arange(P)[:, None], 0.0, -10000.0).astype(np.float32)
    arrays = {
        "x": f("L0_attn_x").reshape(B * N, D),
        "wqkv": np.concatenate([f("L0_attn_Wq").T, f("L0_attn_Wk").T, f("L0_attn_Wv").T], axis=1),
        "wo": f("L0_attn_Wo").T, "bo": f("L0_attn_bo").reshape(1, D),
        "w1": f("L0_ffn_w1"), "b1": f("L0_ffn_b1").T, "w2": f("L0_ffn_w2"), "b2": f("L0_ffn_b2"),
        "cent": f("L0_ffn_centroids"), "wr": f("L0_ffn_w_route"),
        "causal": causal, "head_mask": np.kron(np.eye(P // HD), np.ones((HD, HD))).astype(np.float32),
        "cos": cos, "sin": sin, "tri": np.stack([tri, tri], axis=1), "ident": np.eye(P, dtype=np.float32),
    }
    arrays = {k: np.ascontiguousarray(a) for k, a in arrays.items()}
    nc = bacc.Bacc("TRN2", target_bir_lowering=False, num_devices=1)
    aps = {k: nc.dram_tensor(k, a.shape, mybir.dt.from_np(a.dtype), kind="ExternalInput").ap() for k, a in arrays.items()}
    out = nc.dram_tensor("out", (B * N, D), F32, kind="ExternalOutput").ap()
    layer_kernel(nc, **aps, out=out)
    r = run_bass_kernel_spmd(nc, [arrays], core_ids=[0])
    return r.results[0]["out"].reshape(B, N, D)
```

```python
from contextlib import ExitStack

import concourse.bass as bass
from concourse import mybir

F32 = mybir.dt.float32
BF16 = mybir.dt.bfloat16
F32R = mybir.dt.float32r
I32 = mybir.dt.int32
ALU = mybir.AluOpType
ACT = mybir.ActivationFunctionType
AX = mybir.AxisListType

P = 128
B, N, D = 4, 2048, 256
H, HD = 16, 16
E, F = 8, 128
CH = 512
NC = N // CH
NCH = B * NC
TT = CH // P
KD = D // P
JH = 4
NG = H // JH
NKB = N // P
R = 6
QPART = (0, 0, 1, 1, 0, 2)
KPART = (0, 1, 0, 1, 2, 0)
PRODUCTS = ((0, 0), (0, 1), (1, 0))
SCORE_BOUND = 60.0
WEIGHT_BOUND = 1e6
LEAD = 2


def done(n):
    return n + 1 + LEAD


def two_before(n):
    return n - 1 + LEAD


def wait_alone(eng, semaphore, value, passed):
    eng.wait_ge(semaphore, value)
    eng.sem_inc(passed, 1)


def where(eng, flag, value):
    return eng.If(eng.value_load(flag[0:1, 0:1], min_val=0, max_val=1) == value)


def layer_kernel(nc, x, wqkv, wo, bo, w1, b1, w2, b2, lowest, cent, wr, cos, sin, tri, causal, head_mask, ident, out):
    ctx = ExitStack()
    with ctx:
        def sb(name, shape, dt=F32):
            return ctx.enter_context(nc.sbuf_tensor(name, shape, dt))

        def sem(name):
            return ctx.enter_context(nc.semaphore(name))

        parts_dram = nc.dram_tensor("parts_dram", (3, 2, B, D, N), BF16, kind="Internal").ap()
        v_dram = nc.dram_tensor("v_dram", (B, P, NG, NKB, JH * 2 * HD), F32, kind="Internal").ap()
        att_dram = nc.dram_tensor("att_dram", (NCH, D, CH), F32, kind="Internal").ap()

        bank = ctx.enter_context(nc.psum_tensor("bank", [P, 8, CH], F32))

        ident_sb = sb("ident_sb", [P, P])
        load_const(nc, ctx, sb, sem, ident, ident_sb)
        bounded = sb("bounded", [1, 1], I32)
        shared = [sb(f"shared{u}", [P, HEADS_WORDS]) for u in range(2)]
        groups = [Heads(shared[u], sem(f"b_qkv_loaded{u}")) for u in range(2)]
        chunks = ChunkInputs(shared[0], [sem(f"c_att_loaded{u}") for u in range(2)], x, att_dram)
        parts_stored = [sem(f"a_parts_stored{u}") for u in range(2)]
        v_stored = [sem(f"a_v_stored{u}") for u in range(2)]
        with ExitStack() as s1:
            project(nc, s1, x, wqkv, cos, sin, head_mask, ident_sb, bank, parts_dram, v_dram, groups[0], shared[1],
                    parts_stored, v_stored, bounded)
        weights = ExpertWeights(sb, sem)
        with ExitStack() as s2:
            attend(nc, s2, tri, bounded, bank, parts_dram, v_dram, att_dram, groups, chunks, parts_stored, v_stored, weights,
                   (wo, bo, w1, b1, w2, b2, lowest, cent, wr))
        with ExitStack() as s3:
            attend_unbounded(nc, s3, causal, bounded, ident_sb, bank, parts_dram, v_dram, att_dram, groups, chunks)
        with ExitStack() as s4:
            experts(nc, s4, chunks, weights, shared, ident_sb, bank, out)


def load_const(nc, ctx, sb, sem, ident, ident_sb):
    loaded = sem("ident_loaded")
    with nc.Block() as block:
        @block.sync
        def _(sp):
            sp.dma_start(ident_sb[:], ident).then_inc(loaded, 16)
            sp.wait_ge(loaded, 16)


HEADS_WORDS = JH * N + NKB * JH * 2 * HD


class Heads:
    def __init__(self, memory, loaded):
        half = JH * N // 2
        self.q = memory[0:R * HD, 0:half].bitcast(BF16).rearrange("p (j t) -> p j t", j=JH)
        self.k = memory[0:R * HD, half:2 * half].bitcast(BF16).rearrange("p (j t) -> p j t", j=JH)
        self.v = memory[:, 2 * half:HEADS_WORDS].rearrange("p (k j r) -> p k j r", k=NKB, j=JH)
        self.loaded = loaded


class ChunkInputs:
    def __init__(self, memory, loaded, x, att_dram):
        def part(place):
            return memory[:, place * KD * CH:(place + 1) * KD * CH]

        self.att_sb = [part(u).rearrange("p (k t) -> p k t", k=KD) for u in range(2)]
        self.x_sb = [part(2 + u).rearrange("p (t d) -> p t d", t=TT) for u in range(2)]
        self.loaded, self.x, self.att_dram = loaded, x, att_dram

    def load(self, sp, n, u):
        sp.dma_start(self.att_sb[u], self.att_dram[bass.ds(n, 1)].rearrange("o (k p) t -> p (o k) t", p=P))\
          .then_inc(self.loaded[u], 16)
        sp.dma_start(self.x_sb[u], self.x[bass.ds(n * CH, CH), :].rearrange("(t p) d -> p t d", p=P))\
          .then_inc(self.loaded[u], 16)


LOADS = 2 * R + 1


def load_heads(sp, heads, parts_dram, v_dram, b, g):
    for to, picked, q in ((heads.q, QPART, 0), (heads.k, KPART, 1)):
        for r, part in enumerate(picked):
            sp.dma_start(to[r * HD:(r + 1) * HD, :, :],
                         parts_dram[part, q, bass.ds(b, 1), g * JH * HD:(g + 1) * JH * HD, :]
                         .rearrange("o (j d) t -> d (o j) t", d=HD)).then_inc(heads.loaded, 16)
    sp.dma_start(heads.v.rearrange("p k j r -> p (k j r)"),
                 v_dram[bass.ds(b, 1), :, g].rearrange("o p k r -> (o p) (k r)")).then_inc(heads.loaded, 16)


def project(nc, ctx, x, wqkv, cos, sin, head_mask, ident_sb, bank, parts_dram, v_dram, heads, memory,
            parts_stored, v_stored, bounded):
    def sb(name, shape, dt=F32):
        return ctx.enter_context(nc.sbuf_tensor(name, shape, dt))

    def sem(name):
        return ctx.enter_context(nc.semaphore(name))

    NT = 2 * KD
    w_in = sb("a_w_in", [P, KD, 3 * D])
    w = [sb(f"a_w{i}", [P, KD, 3 * D], F32R) for i in range(2)]
    cos_sb = sb("cos_sb", [P, N])
    sin_sb = sb("sin_sb", [P, N])
    x_sb = [sb(f"a_x{u}", [P, TT, D]) for u in range(2)]
    xn = [sb(f"a_xn{u}", [P, TT, D]) for u in range(2)]
    xnT = [[sb(f"a_xnT{u}{i}", [P, KD, CH], F32R) for i in range(2)] for u in range(2)]
    stats = sb("a_stats", [P, TT, 6])
    mv = sb("a_mv", [P, TT, 2])
    std = sb("a_std", [P, TT, 1])
    rstd = sb("a_rstd", [P, TT, 1])
    shift = sb("a_shift", [P, TT, 1])
    eps = sb("a_eps", [P, 1])
    cosed = [sb(f"a_cosed{q}", [P, KD, CH]) for q in range(2)]
    swapped = [sb(f"a_swapped{q}", [P, KD, CH]) for q in range(2)]
    rot = [sb(f"a_rot{u}", [P, NT, CH]) for u in range(2)]
    rest = sb("a_rest", [P, NT, CH])
    PART_WORDS, V_WORDS = 3 * NT * CH // 2, TT * H * 2 * HD
    parts = [memory[:, u * PART_WORDS:(u + 1) * PART_WORDS].bitcast(BF16).rearrange("p (i q t) -> p i q t", i=3, q=NT)
             for u in range(2)]
    v_sb = [memory[:, 2 * PART_WORDS + u * V_WORDS:2 * PART_WORDS + (u + 1) * V_WORDS]
            .rearrange("p (t h d) -> p t h d", t=TT, h=H) for u in range(2)]

    head_sb = sb("a_head_mask", [P, P])
    gram = sb("a_gram", [P, NT, P])
    row_sums = sb("a_row_sums", [P, NT])
    limits = sb("a_limits", [P, 3])
    largest = sb("a_largest", [1, 3])
    within = sb("a_within", [1, 2])

    passed = sem("a_passed")
    head_loaded = sem("a_head_loaded")
    gram_summed = sem("a_gram_summed")
    gram_step = sem("a_gram_step")
    limits_turned = sem("a_limits_turned")
    weights_loaded = sem("a_weights_loaded")
    x_loaded = [sem(f"a_x_loaded{u}") for u in range(2)]
    consts_set = sem("a_consts_set")
    ln_step = sem("a_ln_step")
    var_ready = sem("a_var_ready")
    std_ready = sem("a_std_ready")
    shift_ready = sem("a_shift_ready")
    halves_ready = sem("a_halves_ready")
    xn_ready = sem("a_xn_ready")
    xnT_summed = sem("a_xnT_summed")
    xnT_high_ready = sem("a_xnT_high_ready")
    xnT_ready = sem("a_xnT_ready")
    w_high_ready = sem("a_w_high_ready")
    w_ready = sem("a_w_ready")
    qk_summed = sem("a_qk_summed")
    v_summed = sem("a_v_summed")
    v_ready = sem("a_v_ready")
    q_step = sem("a_q_step")
    qk_read = [sem("a_q_read"), sem("a_k_read")]
    rope_step = sem("a_rope_step")
    rot_ready = [sem("a_q_rot_ready"), sem("a_k_rot_ready")]
    part0_ready = sem("a_part0_ready")
    rest_ready = sem("a_rest_ready")
    part1_ready = sem("a_part1_ready")
    part2_ready = sem("a_part2_ready")

    LN_STEPS, ROPE_STEPS = 2, 2

    def over_chunks(body, meanwhile=None):
        def run(eng):
            with eng.Fori(0, B - 1) as b:
                for c in range(NC):
                    body(eng, b, c, NC)
            for c in range(NC):
                body(eng, B - 1, c, NC - 1 - c)
                if c == 1 and meanwhile:
                    meanwhile(eng)
        return run

    def halves(b, c):
        return b * (NC // 2) + c // 2 + 1

    with nc.Block() as block:
        @block.sync
        def _(sp):
            def load_x(n, u):
                sp.dma_start(x_sb[u][:], x[bass.ds(n * CH, CH), :].rearrange("(t p) d -> p t d", p=P))\
                  .then_inc(x_loaded[u], 16)

            load_x(0, 0)
            sp.dma_start(w_in[:], wqkv.rearrange("(k p) n -> p k n", p=P)).then_inc(weights_loaded, 16)
            sp.dma_start(cos_sb[:], cos).then_inc(weights_loaded, 16)
            sp.dma_start(sin_sb[:], sin).then_inc(weights_loaded, 16)
            load_x(1, 1)
            sp.dma_start(head_sb[:], head_mask).then_inc(head_loaded, 16)
            sp.wait_ge(xn_ready, 1 + LEAD)
            load_x(2, 0)

            def preload(sp):
                for u in range(2):
                    sp.wait_ge(parts_stored[u], 16 * 6 * (NC // 2 + 1))
                    sp.wait_ge(v_stored[u], 16 * TT * (NC // 2 + 1))
                load_heads(sp, heads, parts_dram, v_dram, 0, 0)

            def body(sp, b, c, ahead):
                n, u = b * NC + c, c % 2
                if ahead >= 3:
                    wait_alone(sp, xn_ready, done(n) + 1, passed)
                    load_x(n + 3, 1 - u)
                wait_alone(sp, v_ready, done(n), passed)
                for t in range(TT):
                    sp.dma_start(v_dram[bass.ds(b, 1), :, :, c * TT + t, :].rearrange("o p g r -> p (o g) r"),
                                 v_sb[u][:, t].rearrange("p (g j) r -> p g (j r)", g=NG)).then_inc(v_stored[u], 16)
                for q in range(2):
                    wait_alone(sp, part2_ready, done(n) * 2 - 1 + q, passed)
                    for i in range(3):
                        sp.dma_start(parts_dram[i, q, bass.ds(b, 1), :, c * CH:(c + 1) * CH]
                                     .rearrange("o (k p) t -> p (o k) t", p=P),
                                     parts[u][:, i, KD * q:KD * (q + 1)]).then_inc(parts_stored[u], 16)

            over_chunks(body, preload)(sp)

        @block.tensor
        def _(pe):
            def transposes(n, u):
                pe.wait_ge(xn_ready, done(n))
                pe.wait_ge(xnT_ready, done(n) - 1)
                for k in range(KD):
                    for t in range(TT):
                        mm = pe.transpose(bank[:, k, t * P:(t + 1) * P], xn[u][:, t, k * P:(k + 1) * P], ident_sb[:])
                mm.then_inc(xnT_summed, 1)

            pe.sem_inc(xnT_summed, LEAD)
            pe.wait_ge(weights_loaded, 48)
            for t in range(NT):
                for k in range(KD):
                    mm = pe.matmul(bank[:, 2 + t, 0:P], w_in[:, k, t * P:(t + 1) * P], w_in[:, k, t * P:(t + 1) * P],
                                   start=(k == 0), stop=(k == KD - 1))
            mm.then_inc(gram_summed, 1)
            transposes(0, 0)
            pe.wait_ge(w_ready, 1)
            pe.wait_ge(gram_step, 1)

            def body(pe, b, c, ahead):
                n, u = b * NC + c, c % 2
                pe.wait_ge(xnT_ready, done(n))
                for t in range(NT):
                    if t % KD == 0:
                        pe.wait_ge(qk_read[t // KD], n + 1)
                    for k in range(KD):
                        for i, (a, z) in enumerate(PRODUCTS):
                            mm = pe.matmul(bank[:, 2 + t, :], w[a][:, k, t * P:(t + 1) * P], xnT[u][z][:, k, :],
                                           start=(k + i == 0), stop=(k == KD - 1 and i == 2))
                    if t % KD == KD - 1:
                        mm.then_inc(qk_summed, 1)
                    if t == KD - 1 and ahead >= 1:
                        transposes(n + 1, 1 - u)
                pe.wait_ge(v_ready, done(n) - 1)
                for t in range(TT):
                    for k in range(KD):
                        for i, (a, z) in enumerate(PRODUCTS):
                            mm = pe.matmul(bank[:, 6 + t // 2, (t % 2) * D:(t % 2 + 1) * D],
                                           xnT[u][a][:, k, t * P:(t + 1) * P], w[z][:, k, 2 * D:3 * D],
                                           start=(k + i == 0), stop=(k == KD - 1 and i == 2))
                mm.then_inc(v_summed, 1)

            over_chunks(body)(pe)
            pe.wait_ge(gram_step, 4)
            for j in range(3):
                mm = pe.transpose(bank[0:1, 0, j * P:(j + 1) * P], limits[:, j:j + 1], ident_sb[:])
            mm.then_inc(limits_turned, 1)

        @block.scalar
        def _(act):
            act.sem_inc(v_ready, LEAD)
            act.sem_inc(xn_ready, LEAD)
            act.wait_ge(weights_loaded, 48)
            nc.scalar.copy(w[0][:], w_in[:]).then_inc(w_high_ready, 1)

            def spread(n):
                act.wait_ge(var_ready, n + 1)
                nc.scalar.activation(std[:], mv[:, :, 1:2], ACT.Sqrt, bias=eps[:, 0:1]).then_inc(std_ready, 1)

            def normed(n, u):
                act.wait_ge(shift_ready, n + 1)
                act.wait_ge(xnT_summed, two_before(n))
                for t in range(TT):
                    ins = nc.scalar.activation(xn[u][:, t], x_sb[u][:, t], ACT.Identity, bias=shift[:, t],
                                               scale=rstd[:, t])
                ins.then_inc(xn_ready, 1)

            def turned(n, u):
                act.wait_ge(xnT_summed, done(n))
                nc.scalar.copy(xnT[u][0][:], bank[:, 0:KD, :]).then_inc(xnT_high_ready, 1)

            def part(i, n, u, q):
                of = slice(KD * q, KD * (q + 1))
                if i == 0:
                    act.wait_ge(rot_ready[q], n + 2)
                    nc.scalar.copy(parts[u][:, 0, of], rot[u][:, of]).then_inc(part0_ready, 1)
                else:
                    act.wait_ge(rest_ready, n * 2 + q + 1)
                    nc.scalar.copy(parts[u][:, 1, of], rest[:, of]).then_inc(part1_ready, 1)

            def q_parts(n, u, earlier):
                act.wait_ge(parts_stored[u], 16 * 6 * earlier)
                part(0, n, u, 0)

            act.wait_ge(consts_set, 3)
            spread(0)
            normed(0, 0)
            spread(1)
            turned(0, 0)
            normed(1, 1)
            spread(2)
            turned(1, 1)
            q_parts(0, 0, 1)
            part(1, 0, 0, 0)

            def body(act, b, c, ahead):
                n, u = b * NC + c, c % 2
                if ahead >= 2:
                    normed(n + 2, u)
                act.wait_ge(v_summed, n + 1)
                act.wait_ge(v_stored[u], 16 * TT * halves(b, c))
                for a in range(2):
                    ins = nc.scalar.copy(v_sb[u][:, 2 * a:2 * a + 2, :, 0:HD],
                                         bank[:, 6 + a, :].rearrange("p (t h d) -> p t h d", t=2, h=H))
                ins.then_inc(v_ready, 1)
                part(0, n, u, 1)
                part(1, n, u, 1)
                if ahead >= 3:
                    spread(n + 3)
                if ahead >= 2:
                    turned(n + 2, u)
                if ahead >= 1:
                    q_parts(n + 1, 1 - u, halves(b, c + 1))
                    part(1, n + 1, 1 - u, 0)

            over_chunks(body)(act)

        @block.gpsimd
        def _(pool):
            nc.gpsimd.memset(eps[:], 1e-5).then_inc(consts_set, 1)
            pool.sem_inc(part2_ready, LEAD * 2)
            pool.sem_inc(rot_ready[1], 1)
            for u in range(2):
                nc.gpsimd.memset(v_sb[u][:, :, :, HD:2 * HD], 1.0).then_inc(consts_set, 1)
                pool.sem_inc(parts_stored[u], 16 * 6)
                pool.sem_inc(v_stored[u], 16 * TT)

            def rests(n, u, q):
                of = slice(KD * q, KD * (q + 1))
                pool.wait_ge(part0_ready, n * 2 + q + 1)
                nc.gpsimd.tensor_tensor(rest[:, of], rot[u][:, of], parts[u][:, 0, of],
                                        ALU.subtract).then_inc(rest_ready, 1)

            def last_part(n, u, q):
                of = slice(KD * q, KD * (q + 1))
                pool.wait_ge(part1_ready, n * 2 + q + 1)
                nc.gpsimd.tensor_tensor(parts[u][:, 2, of], rest[:, of], parts[u][:, 1, of],
                                        ALU.subtract).then_inc(part2_ready, 1)

            def beginning(n, u):
                rests(n, u, 0)
                pool.wait_ge(halves_ready, n + 2)
                nc.gpsimd.tensor_tensor(rot[u][:, KD:], cosed[1][:], swapped[1][:], ALU.add).then_inc(rot_ready[1], 1)
                last_part(n, u, 0)

            beginning(0, 0)

            def body(pool, b, c, ahead):
                n, u = b * NC + c, c % 2
                rests(n, u, 1)
                last_part(n, u, 1)
                if ahead >= 1:
                    beginning(n + 1, 1 - u)

            over_chunks(body)(pool)

        @block.vector
        def _(dve):
            dve.sem_inc(rot_ready[0], 1)
            dve.sem_inc(halves_ready, 1)
            for q in range(2):
                dve.sem_inc(qk_read[q], 1)
            dve.sem_inc(xnT_ready, LEAD)

            def statistics(n, loads, u):
                dve.wait_ge(x_loaded[u], 16 * loads)
                for t in range(TT):
                    ins = nc.vector.bn_stats(stats[:, t], x_sb[u][:, t])
                ins.then_inc(ln_step, 1)
                wait_alone(dve, ln_step, n * LN_STEPS + 1, passed)
                for t in range(TT):
                    ins = nc.vector.bn_aggr(mv[:, t], stats[:, t])
                ins.then_inc(var_ready, 1)

            def factors(n):
                dve.wait_ge(std_ready, n + 1)
                dve.wait_ge(xn_ready, done(n) - 1)
                nc.vector.reciprocal(rstd[:], std[:]).then_inc(ln_step, 1)
                dve.wait_ge(ln_step, n * LN_STEPS + 2)
                nc.vector.scalar_tensor_tensor(out=shift[:], in0=mv[:, :, 0:1], scalar=-1.0, in1=rstd[:],
                                               op0=ALU.mult, op1=ALU.mult).then_inc(shift_ready, 1)

            def lows(n, u):
                dve.wait_ge(xnT_high_ready, n + 1)
                nc.vector.tensor_tensor(xnT[u][1][:], bank[:, 0:KD, :], xnT[u][0][:].bitcast(F32),
                                        ALU.subtract).then_inc(xnT_ready, 1)

            def rotate(n, u, c, q):
                def table(of_angles):
                    return of_angles[:, c * CH:(c + 1) * CH].unsqueeze(1).to_broadcast([P, KD, CH])

                wait_alone(dve, qk_summed, n * 2 + q + 1, passed)
                nc.vector.stream_shuffle(swapped[q][:], bank[:, 2 + KD * q:2 + KD * (q + 1), :],
                                         [i ^ 1 for i in range(32)]).then_inc(rope_step, 1)
                nc.vector.tensor_tensor(cosed[q][:], bank[:, 2 + KD * q:2 + KD * (q + 1), :], table(cos_sb),
                                        ALU.mult).then_inc(qk_read[q], 1)
                dve.wait_ge(rope_step, n * ROPE_STEPS + q + 1)
                ins = nc.vector.tensor_tensor(swapped[q][:], swapped[q][:], table(sin_sb), ALU.mult)
                if q == 1:
                    ins.then_inc(halves_ready, 1)
                    return
                ins.then_inc(q_step, 1)
                dve.wait_ge(q_step, n + 1)
                nc.vector.tensor_tensor(rot[u][:, 0:KD], cosed[0][:], swapped[0][:], ALU.add).then_inc(rot_ready[0], 1)

            statistics(0, 1, 0)
            factors(0)
            dve.wait_ge(w_high_ready, 1)
            nc.vector.tensor_tensor(w[1][:], w_in[:], w[0][:].bitcast(F32), ALU.subtract).then_inc(w_ready, 1)
            statistics(1, 1, 1)
            factors(1)
            lows(0, 0)
            dve.wait_ge(gram_summed, 1)
            dve.wait_ge(head_loaded, 16)
            nc.vector.tensor_tensor(gram[:], bank[:, 2:2 + NT, 0:P], head_sb[:].unsqueeze(1).to_broadcast([P, NT, P]),
                                    ALU.mult).then_inc(gram_step, 1)
            nc.vector.tensor_reduce(limits[:, 2:3], w_in[:].rearrange("p k n -> p (k n)"), AX.X, ALU.max,
                                    apply_absolute_value=True).then_inc(gram_step, 1)
            dve.wait_ge(gram_step, 1)
            nc.vector.tensor_reduce(row_sums[:], gram[:], AX.X, ALU.add, apply_absolute_value=True).then_inc(gram_step, 1)
            dve.wait_ge(gram_step, 3)
            nc.vector.tensor_reduce(limits[:, 0:2], row_sums[:].rearrange("p (q k) -> p q k", q=2), AX.X, ALU.max)\
              .then_inc(gram_step, 1)

            def body(dve, b, c, ahead):
                n, u = b * NC + c, c % 2
                if ahead >= 2:
                    statistics(n + 2, halves(b, c) + 1, u)
                dve.wait_ge(part2_ready, two_before(n) * 2)
                rotate(n, u, c, 0)
                if ahead >= 1:
                    lows(n + 1, 1 - u)
                if ahead >= 2:
                    factors(n + 2)
                dve.wait_ge(rot_ready[1], n + 1)
                rotate(n, u, c, 1)

            over_chunks(body)(dve)
            dve.wait_ge(limits_turned, 1)
            nc.vector.tensor_reduce(largest[:], bank[0:1, 0, 0:3 * P].rearrange("p (j r) -> p j r", j=3), AX.X, ALU.max)\
              .then_inc(gram_step, 1)
            dve.wait_ge(gram_step, 5)
            nc.vector.tensor_tensor(within[:, 0:1], largest[:, 0:1], largest[:, 1:2], ALU.mult)
            nc.vector.tensor_scalar(within[:, 1:2], largest[:, 2:3], WEIGHT_BOUND, None, ALU.is_le).then_inc(gram_step, 1)
            dve.wait_ge(gram_step, 6)
            nc.vector.tensor_scalar(largest[:, 0:1], within[:, 0:1], (SCORE_BOUND * HD / D) ** 2, None, ALU.is_le)\
              .then_inc(gram_step, 1)
            dve.wait_ge(gram_step, 7)
            nc.vector.tensor_tensor(bounded[:], largest[:, 0:1], within[:, 1:2], ALU.mult).then_inc(gram_step, 1)
            dve.wait_ge(gram_step, 8)


class ExpertWeights:
    def __init__(self, sb, sem):
        self.wo_sb = [sb(f"c_wo{i}", [P, KD, D], F32R) for i in range(2)]
        self.bo_sb = sb("c_bo", [P, TT, D])
        self.w1_sb = [sb(f"c_w1{i}", [P, KD, E, F], F32R) for i in range(2)]
        self.b1_sb = sb("c_b1", [P, E])
        self.w2_sb = [sb(f"c_w2{i}", [P, E, D], F32R) for i in range(2)]
        self.b2_in = sb("c_b2_in", [3 * E, D])
        self.lowest_sb = sb("c_lowest", [3 * E, 1])
        self.b2_high = sb("c_b2_high", [3 * E, D], F32R)
        self.b2_sb = sb("c_b2", [3 * E, D], F32R)
        self.cent_sb = sb("c_cent", [E, D])
        self.cent_sq = sb("c_cent_sq", [E, D])
        self.cent_n = sb("c_cent_n", [E, 1])
        self.cent_s = sb("c_cent_s", [E, 1])
        self.cent_half = sb("c_cent_half", [E, 1])
        self.wr_sb = sb("c_wr", [E, D])

        self.loaded = sem("c_weights_loaded")
        self.cent_loaded = sem("c_cent_loaded")
        self.cent_step = sem("c_cent_step")
        self.half_set = sem("c_cent_half_set")
        self.cent_rooted = sem("c_cent_rooted")
        self.high_ready = sem("c_weights_high_ready")
        self.low_ready = sem("c_weights_low_ready")

    def inputs(self, sb):
        self.wo_in = sb("c_wo_in", [P, KD, D])
        self.w1_in = sb("c_w1_in", [P, KD, E, F])
        self.w2_in = sb("c_w2_in", [P, E, D])

    def load(self, sp, tri_sb, tri, tri_loaded, wo, bo, w1, b1, w2, b2, lowest, cent, wr):
        sp.dma_start(self.cent_sb[:], cent).then_inc(self.cent_loaded, 16)
        sp.dma_start(tri_sb[:], tri).then_inc(tri_loaded, 16)
        transfers = [(self.wr_sb[:], wr), (self.wo_in[:], wo.rearrange("(k p) n -> p k n", p=P)),
                     (self.w1_in[:, 0], w1[:, 0:P, :].rearrange("e p f -> p e f")),
                     (self.w1_in[:, 1], w1[:, P:D, :].rearrange("e p f -> p e f")), (self.b1_sb[:], b1),
                     (self.w2_in[:], w2.rearrange("e f d -> f e d")), (self.lowest_sb[:], lowest)]
        transfers += [(self.b2_in[r * E:(r + 1) * E, :], b2) for r in range(3)]
        transfers += [(self.bo_sb[:, t], bo.partition_broadcast(P)) for t in range(TT)]
        for to, source in transfers:
            sp.dma_start(to, source).then_inc(self.loaded, 16)
        self.count = len(transfers)

    def prepare(self, nc, dve):
        dve.wait_ge(self.cent_loaded, 16)
        nc.vector.tensor_tensor(self.cent_sq[:], self.cent_sb[:], self.cent_sb[:], ALU.mult).then_inc(self.cent_step, 1)
        dve.wait_ge(self.cent_step, 1)
        nc.vector.tensor_reduce(self.cent_n[:], self.cent_sq[:], AX.X, ALU.add).then_inc(self.cent_step, 1)
        dve.wait_ge(self.loaded, 16 * self.count)
        nc.vector.tensor_copy(self.wo_sb[0][:], self.wo_in[:])
        nc.vector.tensor_copy(self.w1_sb[0][:], self.w1_in[:])
        nc.vector.tensor_copy(self.w2_sb[0][:], self.w2_in[:])
        nc.vector.tensor_copy(self.b2_high[:], self.b2_in[:]).then_inc(self.high_ready, 1)
        dve.wait_ge(self.high_ready, 1)
        nc.vector.tensor_tensor(self.wo_sb[1][:], self.wo_in[:], self.wo_sb[0][:].bitcast(F32), ALU.subtract)
        nc.vector.tensor_tensor(self.w1_sb[1][:], self.w1_in[:], self.w1_sb[0][:].bitcast(F32), ALU.subtract)
        nc.vector.tensor_tensor(self.w2_sb[1][:], self.w2_in[:], self.w2_sb[0][:].bitcast(F32), ALU.subtract)
        nc.vector.scalar_tensor_tensor(out=self.b2_sb[:], in0=self.b2_high[:].bitcast(F32), scalar=self.lowest_sb[:, 0:1],
                                       in1=self.b2_in[:], op0=ALU.mult, op1=ALU.add).then_inc(self.low_ready, 1)
        dve.wait_ge(self.cent_rooted, 1)
        nc.vector.tensor_scalar(self.cent_s[:], self.cent_s[:], 1e-12, None, ALU.max).then_inc(self.cent_rooted, 1)
        dve.wait_ge(self.cent_rooted, 2)
        nc.vector.reciprocal(self.cent_n[:], self.cent_s[:]).then_inc(self.cent_step, 1)
        dve.wait_ge(self.cent_step, 3)
        nc.vector.tensor_scalar(self.cent_sb[:], self.cent_sb[:], self.cent_n[:, 0:1], None, ALU.mult).then_inc(self.cent_step, 1)

    def root(self, nc, pool):
        nc.gpsimd.memset(self.cent_half[:], 0.5).then_inc(self.half_set, 1)
        pool.wait_ge(self.half_set, 1)
        pool.wait_ge(self.cent_step, 2)
        nc.gpsimd.tensor_tensor(self.cent_s[:], self.cent_n[:], self.cent_half[:], ALU.pow).then_inc(self.cent_rooted, 1)


def attend(nc, ctx, tri, bounded, bank, parts_dram, v_dram, att_dram, groups, chunks, parts_stored, v_stored, weights,
           weight_sources):
    def sb(name, shape, dt=F32):
        return ctx.enter_context(nc.sbuf_tensor(name, shape, dt))

    def sem(name):
        return ctx.enter_context(nc.semaphore(name))

    q_sb, k_sb, v_sb = [x.q for x in groups], [x.k for x in groups], [x.v for x in groups]
    weights.inputs(sb)
    tri_sb = sb("b_tri", [P, 2, P])
    PB = 8
    probs = [sb(f"b_probs{i}", [P, 2, CH]) for i in range(PB)]
    o_sb = [sb(f"b_o{i}", [P, CH]) for i in range(2)]
    sums = sb("b_sums", [P, CH])
    o_norm = [sb(f"b_on{i}", [P, CH]) for i in range(2)]

    passed = sem("b_passed")
    tri_loaded = sem("b_tri_loaded")
    qkv_loaded = [x.loaded for x in groups]
    scores_summed = sem("b_scores_summed")
    probs_ready = sem("b_probs_ready")
    probs_masked = sem("b_probs_masked")
    steps_summed = sem("b_steps_summed")
    o_copied = sem("b_o_copied")
    norm_step = sem("b_norm_step")
    o_ready = sem("b_o_ready")
    o_stored = [sem(f"b_o_stored{i}") for i in range(2)]

    steps = [(c, kb) for c in range(NC) for kb in range((c + 1) * TT)]
    GS = len(steps)
    body_steps = [(u, c, kb) for u in range(2) for c, kb in steps]
    SB = len(body_steps)
    on_diagonal = [kb >= c * TT for _, c, kb in body_steps]
    MB = 2 * sum(on_diagonal)
    last_of_chunk = [kb == (c + 1) * TT - 1 for _, c, kb in body_steps]

    def slot(m):
        return bank[:, 2 * (m % 3):2 * (m % 3) + 2, :]

    def first_column(c, kb):
        return max(0, kb - c * TT) * P

    with nc.Block() as block:
        @block.sync
        def _(sp):
            weights.load(sp, tri_sb, tri, tri_loaded, *weight_sources)
            for u in range(2):
                sp.wait_ge(v_stored[u], 16 * TT * (NCH // 2 + 1))
                sp.wait_ge(parts_stored[u], 16 * 6 * (NCH // 2 + 1))
            with where(sp, bounded, 1):
                def stores(b, g):
                    for c in range(NC):
                        k = c % 2
                        wait_alone(sp, o_ready, done(b * NG * NC + g * NC + c), passed)
                        for j in range(JH):
                            row = (g * JH + j) * HD
                            sp.dma_start(att_dram[bass.ds(b * NC + c, 1), row:row + HD, :].rearrange("o d t -> (o d) t"),
                                         o_norm[k][j * 2 * HD:j * 2 * HD + HD, :]).then_inc(o_stored[k], 16)

                for u in range(2):
                    sp.sem_inc(o_stored[u], 16 * JH)
                load_heads(sp, groups[1], parts_dram, v_dram, 0, 1)

                def sequence(b, last):
                    for g in range(NG):
                        stores(b, g)
                        if g + 2 < NG or not last:
                            wait_alone(sp, steps_summed, (b * NG + g + 1) * GS, passed)
                            load_heads(sp, groups[g % 2], parts_dram, v_dram, b + (g + 2) // NG, (g + 2) % NG)
                        if g == NG - 2 and last:
                            sp.wait_ge(steps_summed, (b * NG + g + 1) * GS)
                            for k in range(2):
                                sp.wait_ge(o_stored[k], 16 * JH * (NG * NC // 2 + 1))
                            for n in range(2):
                                chunks.load(sp, n, n)

                with sp.Fori(0, B - 1) as b:
                    sequence(b, False)
                sequence(B - 1, True)
                for k in range(2):
                    sp.wait_ge(o_stored[k], 16 * JH * (B * NG * NC // 2 + 1))

        @block.tensor
        def _(pe):
            with where(pe, bounded, 1):
                with pe.Fori(0, B * NG // 2) as i:
                    def scores(m):
                        u, c, kb = body_steps[m // 2]
                        if m % (2 * GS) == 0:
                            pe.wait_ge(qkv_loaded[u], 16 * LOADS * (i + 1))
                        if m >= 3:
                            pe.wait_ge(probs_ready, i * 2 * SB + m - 2)
                        off = first_column(c, kb)
                        for h in range(2):
                            j = 2 * (m % 2) + h
                            mm = pe.matmul(slot(m)[:, h, off:CH], k_sb[u][:, j, kb * P:(kb + 1) * P],
                                           q_sb[u][:, j, c * CH + off:(c + 1) * CH], start=True, stop=True)
                        mm.then_inc(scores_summed, 1)

                    def outputs(n):
                        u, c, kb = body_steps[n]
                        if on_diagonal[n]:
                            pe.wait_ge(probs_masked, i * MB + 2 * sum(on_diagonal[:n + 1]))
                        else:
                            pe.wait_ge(probs_ready, i * 2 * SB + 2 * n + 2)
                        if kb == 0:
                            pe.wait_ge(o_copied, two_before(i * 2 * NC + u * NC + c))
                        off = first_column(c, kb)
                        for j in range(JH):
                            mm = pe.matmul(bank[2 * HD * j:2 * HD * (j + 1), 6 + c % 2, off:CH], v_sb[u][:, kb, j, :],
                                           probs[(2 * n + j // 2) % PB][:, j % 2, off:CH],
                                           start=(kb == 0), stop=last_of_chunk[n])
                        mm.then_inc(steps_summed, 1)

                    scores(0)
                    scores(1)
                    scores(2)
                    for n in range(SB):
                        if n + 1 < SB:
                            scores(2 * n + 3)
                        if n >= 1:
                            outputs(n - 1)
                        if n + 2 < SB:
                            scores(2 * n + 4)
                    outputs(SB - 1)

        @block.scalar
        def _(act):
            with where(act, bounded, 1):
                with act.Fori(0, B * NG // 2) as i:
                    for m in range(2 * SB):
                        u, c, kb = body_steps[m // 2]
                        act.wait_ge(scores_summed, i * 2 * SB + m + 1)
                        if m >= PB:
                            act.wait_ge(steps_summed, i * SB + (m - PB) // 2 + 1)
                        off = first_column(c, kb)
                        nc.scalar.activation(probs[m % PB][:, :, off:CH], slot(m)[:, :, off:CH], ACT.Exp,
                                             scale=1.0 / HD).then_inc(probs_ready, 1)

        @block.gpsimd
        def _(pool):
            weights.root(nc, pool)
            with where(pool, bounded, 1):
                pool.wait_ge(tri_loaded, 16)
                with pool.Fori(0, B * NG // 2) as i:
                    for m in range(2 * SB):
                        u, c, kb = body_steps[m // 2]
                        if on_diagonal[m // 2]:
                            off = first_column(c, kb)
                            pool.wait_ge(probs_ready, i * 2 * SB + m + 1)
                            nc.gpsimd.tensor_tensor(probs[m % PB][:, :, off:off + P], probs[m % PB][:, :, off:off + P],
                                                    tri_sb[:], ALU.mult).then_inc(probs_masked, 1)

        @block.vector
        def _(dve):
            dve.sem_inc(o_copied, LEAD)
            dve.sem_inc(o_ready, LEAD)
            weights.prepare(nc, dve)
            with where(dve, bounded, 1):
                with dve.Fori(0, B * NG // 2) as i:
                    for n in range(SB):
                        if not last_of_chunk[n]:
                            continue
                        u, c, _ = body_steps[n]
                        k, q = c % 2, u * NC + c
                        dve.wait_ge(steps_summed, i * SB + n + 1)
                        nc.vector.tensor_copy(o_sb[k][:], bank[:, 6 + k, :]).then_inc(o_copied, 1)
                        wait_alone(dve, o_copied, done(i * 2 * NC + q), passed)
                        nc.vector.stream_shuffle(sums[:], o_sb[k][:], [HD + r % HD for r in range(2 * HD)])\
                          .then_inc(norm_step, 1)
                        dve.wait_ge(norm_step, i * 4 * NC + 2 * q + 1)
                        nc.vector.reciprocal(sums[:], sums[:]).then_inc(norm_step, 1)
                        dve.wait_ge(norm_step, i * 4 * NC + 2 * q + 2)
                        dve.wait_ge(o_stored[k], 16 * JH * (i * NC + q // 2 + 1))
                        nc.vector.tensor_tensor(o_norm[k][:], o_sb[k][:], sums[:], ALU.mult).then_inc(o_ready, 1)


def attend_unbounded(nc, ctx, causal, bounded, ident_sb, bank, parts_dram, v_dram, att_dram, groups, chunks):
    def sb(name, shape, dt=F32):
        return ctx.enter_context(nc.sbuf_tensor(name, shape, dt))

    def sem(name):
        return ctx.enter_context(nc.semaphore(name))

    q_sb, k_sb, v_sb = groups[1].q, groups[1].k, groups[1].v
    causal_sb = sb("g_causal", [P, 2 * N - P])
    scores = sb("g_scores", [P, N])
    top = sb("g_top", [P, 1])
    minus_top = sb("g_minus_top", [P, 1])
    probs = sb("g_probs", [P, N])
    probsT = sb("g_probsT", [P, N])
    o_sb = sb("g_o", [2 * HD, P])
    sums = sb("g_sums", [2 * HD, P])
    o_norm = sb("g_on", [2 * HD, P])

    passed = sem("g_passed")
    causal_loaded = sem("g_causal_loaded")
    qkv_loaded = sem("g_qkv_loaded")
    scores_summed = sem("g_scores_summed")
    scores_masked = sem("g_scores_masked")
    top_found = sem("g_top_found")
    top_negated = sem("g_top_negated")
    probs_ready = sem("g_probs_ready")
    probs_turned = sem("g_probs_turned")
    probsT_ready = sem("g_probsT_ready")
    o_summed = sem("g_o_summed")
    o_copied = sem("g_o_copied")
    sums_beside = sem("g_sums_beside")
    inverted = sem("g_inverted")
    o_ready = sem("g_o_ready")
    o_stored = sem("g_o_stored")

    GT = JH * NKB

    def over_tiles(eng, group, tile):
        with eng.Fori(0, B) as b:
            with eng.Fori(0, NG) as g:
                i = b * NG + g
                group(b, g, i)
                for j in range(JH):
                    with eng.Fori(0, NC) as c:
                        for s in range(TT):
                            tile(b, g, j, c, s, i * GT + j * NKB + c * TT + s)

    def none(b, g, i):
        pass

    with nc.Block() as block:
        @block.sync
        def _(sp):
            with where(sp, bounded, 0):
                sp.dma_start(causal_sb[:], causal).then_inc(causal_loaded, 16)
                sp.sem_inc(o_stored, 16)

                def load(b, g, i):
                    wait_alone(sp, o_stored, 16 * (i * GT + 1), passed)
                    for to, picked, q in ((q_sb, QPART, 0), (k_sb, KPART, 1)):
                        for r, part in enumerate(picked):
                            sp.dma_start(to[r * HD:(r + 1) * HD, :, :],
                                         parts_dram[part, q, bass.ds(b, 1), bass.ds(g * JH * HD, JH * HD), :]
                                         .rearrange("o (j d) t -> d (o j) t", d=HD)).then_inc(qkv_loaded, 16)
                    sp.dma_start(v_sb.rearrange("p k j r -> p (k j r)"),
                                 v_dram[bass.ds(b, 1), :, bass.ds(g, 1)].rearrange("o p e k r -> (o p e) (k r)"))\
                      .then_inc(qkv_loaded, 16)

                def store(b, g, j, c, s, n):
                    wait_alone(sp, o_ready, n + 1, passed)
                    sp.dma_start(att_dram[bass.ds(b * NC + c, 1), bass.ds(g * JH * HD + j * HD, HD), s * P:(s + 1) * P]
                                 .rearrange("o d t -> (o d) t"), o_norm[0:HD, :]).then_inc(o_stored, 16)

                over_tiles(sp, load, store)
                sp.wait_ge(o_stored, 16 * (B * NG * GT + 1))
                sp.wait_ge(groups[0].loaded, 16 * LOADS)
                for n in range(2):
                    chunks.load(sp, n, n)

        @block.tensor
        def _(pe):
            with where(pe, bounded, 0):
                def loaded(b, g, i):
                    wait_alone(pe, qkv_loaded, 16 * LOADS * (i + 1), passed)

                def tile(b, g, j, c, s, n):
                    for k in range(NC):
                        mm = pe.matmul(bank[:, k, :], q_sb[:, j, bass.ds(c * CH + s * P, P)],
                                       k_sb[:, j, k * CH:(k + 1) * CH], start=True, stop=True)
                    mm.then_inc(scores_summed, 1)
                    pe.wait_ge(probs_ready, n + 1)
                    for k in range(NKB):
                        mm = pe.transpose(bank[:, k // TT, k % TT * P:(k % TT + 1) * P], probs[:, k * P:(k + 1) * P],
                                          ident_sb[:])
                    mm.then_inc(probs_turned, 1)
                    pe.wait_ge(probsT_ready, n + 1)
                    for k in range(NKB):
                        mm = pe.matmul(bank[0:2 * HD, 4, 0:P], v_sb[:, k, j, :], probsT[:, k * P:(k + 1) * P],
                                       start=(k == 0), stop=(k == NKB - 1))
                    mm.then_inc(o_summed, 1)

                over_tiles(pe, loaded, tile)

        @block.scalar
        def _(act):
            with where(act, bounded, 0):
                def tile(b, g, j, c, s, n):
                    act.wait_ge(top_negated, n + 1)
                    nc.scalar.activation(probs[:], scores[:], ACT.Exp, bias=minus_top[:, 0:1]).then_inc(probs_ready, 1)
                    act.wait_ge(probs_turned, n + 1)
                    nc.scalar.copy(probsT[:].rearrange("p (k t) -> p k t", k=NC), bank[:, 0:NC, :])\
                      .then_inc(probsT_ready, 1)

                over_tiles(act, none, tile)

        @block.vector
        def _(dve):
            with where(dve, bounded, 0):
                dve.wait_ge(causal_loaded, 16)

                def tile(b, g, j, c, s, n):
                    wait_alone(dve, scores_summed, n + 1, passed)
                    nc.vector.scalar_tensor_tensor(
                        out=scores[:].rearrange("p (k t) -> p k t", k=NC), in0=bank[:, 0:NC, :], scalar=1.0 / HD,
                        in1=causal_sb[:, bass.ds(N - P - s * P - c * CH, N)].rearrange("p (k t) -> p k t", k=NC),
                        op0=ALU.mult, op1=ALU.add).then_inc(scores_masked, 1)
                    dve.wait_ge(scores_masked, n + 1)
                    nc.vector.tensor_reduce(top[:], scores[:], AX.X, ALU.max).then_inc(top_found, 1)
                    dve.wait_ge(top_found, n + 1)
                    nc.vector.tensor_scalar(minus_top[:], top[:], -1.0, None, ALU.mult).then_inc(top_negated, 1)
                    dve.wait_ge(o_summed, n + 1)
                    nc.vector.tensor_copy(o_sb[:], bank[0:2 * HD, 4, 0:P]).then_inc(o_copied, 1)
                    wait_alone(dve, o_copied, n + 1, passed)
                    nc.vector.stream_shuffle(sums[:], o_sb[:], [HD + r % HD for r in range(2 * HD)])\
                      .then_inc(sums_beside, 1)
                    dve.wait_ge(sums_beside, n + 1)
                    nc.vector.reciprocal(sums[:], sums[:]).then_inc(inverted, 1)
                    dve.wait_ge(inverted, n + 1)
                    dve.wait_ge(o_stored, 16 * (n + 1))
                    nc.vector.tensor_tensor(o_norm[:], o_sb[:], sums[:], ALU.mult).then_inc(o_ready, 1)

                over_tiles(dve, none, tile)


def experts(nc, ctx, chunks, weights, shared, ident_sb, bank, out):
    def sb(name, shape, dt=F32):
        return ctx.enter_context(nc.sbuf_tensor(name, shape, dt))

    def sem(name):
        return ctx.enter_context(nc.semaphore(name))

    wo_sb, bo_sb, w1_sb, b1_sb, w2_sb, b2_sb = (
        weights.wo_sb, weights.bo_sb, weights.w1_sb, weights.b1_sb, weights.w2_sb, weights.b2_sb)
    cent_sb, wr_sb = weights.cent_sb, weights.wr_sb
    route = sb("c_route", [P, KD, 32])
    minus_half = sb("c_minus_half", [P, TT])
    half = sb("c_half", [P, TT])
    def from_shared(place):
        memory, size = shared[place // 8], TT * D
        place %= 8
        return memory[:, place * size:(place + 1) * size].rearrange("p (t d) -> p t d", t=TT)

    att_sb, x_sb = chunks.att_sb, chunks.x_sb
    att = [[sb(f"c_att{u}{i}", [P, KD, CH], F32R) for i in range(2)] for u in range(2)]
    x2 = [from_shared(4 + u) for u in range(2)]
    xn = [from_shared(10 + u) for u in range(2)]
    xnT32 = [from_shared(12 + u).rearrange("p t d -> p (t d)").rearrange("p (k t) -> p k t", k=KD) for u in range(2)]
    xnT = [[sb(f"c_xnT{u}{i}", [P, KD, CH], F32R) for i in range(2)] for u in range(2)]
    scoresT = sb("c_scoresT", [P, P])
    stats = sb("c_stats", [P, TT, 6])
    mv = sb("c_mv", [P, TT, 2])
    var_eps = sb("c_var_eps", [P, TT])
    rstd = sb("c_rstd", [P, TT])
    sq = sb("c_sq", [P, TT])
    root = sb("c_root", [P, TT])
    length = [sb(f"c_length{u}", [P, TT]) for u in range(2)]
    scored = sb("c_scored", [P, TT, 2 * E])
    logits = sb("c_logits", [P, TT, E])
    top = sb("c_top", [P, TT, 8])
    shifted = sb("c_shifted", [P, TT, E])
    kept = sb("c_kept", [P, TT, E])
    exps = sb("c_exps", [P, TT, E])
    total = sb("c_total", [P, TT])
    gates = [sb(f"c_gates{u}", [P, TT, E]) for u in range(2)]
    gate_halves = sb("c_gate_halves", [P, TT, 3 * E], F32R)
    gatesT = sb("c_gatesT", [3 * E, CH], F32R)
    HB = 4
    hid32 = [shared[1][:, (12 + i) * CH:(13 + i) * CH] for i in range(HB)]
    hid = [sb(f"c_hid{i}", [P, E, CH], F32R) for i in range(2)]
    acc = [from_shared(6 + u) for u in range(2)]
    y = [from_shared(8 + u) for u in range(2)]

    passed = sem("c_passed")
    att_loaded = chunks.loaded
    out_stored = [sem(f"c_out_stored{u}") for u in range(2)]
    consts_set = sem("c_consts_set")
    routeT_summed = sem("c_routeT_summed")
    route_ready = sem("c_route_ready")
    o_summed = sem("c_o_summed")
    x_added = sem("c_x_added")
    x2_ready = sem("c_x2_ready")
    ln_step = sem("c_ln_step")
    var_ready = sem("c_var_ready")
    rstd_ready = sem("c_rstd_ready")
    xn_ready = sem("c_xn_ready")
    length_ready = sem("c_length_ready")
    xnT_summed = sem("c_xnT_summed")
    xnT_high_ready = sem("c_xnT_high_ready")
    xnT_ready = sem("c_xnT_ready")
    att_high = sem("c_att_high")
    att_ready = sem("c_att_ready")
    scoresT_summed = sem("c_scoresT_summed")
    scoresT_ready = sem("c_scoresT_ready")
    hid32_ready = sem("c_hid32_ready")
    hid_high = sem("c_hid_high")
    scores_summed = sem("c_scores_summed")
    gate_step = sem("c_gate_step")
    exps_ready = sem("c_exps_ready")
    gates_ready = sem("c_gates_ready")
    gates_high = sem("c_gates_high")
    gate_halves_ready = sem("c_gate_halves_ready")
    gatesT_summed = sem("c_gatesT_summed")
    gatesT_ready = sem("c_gatesT_ready")
    hid_summed = sem("c_hid_summed")
    hid_ready = sem("c_hid_ready")
    y_summed = sem("c_y_summed")
    y_added = sem("c_y_added")

    Y_BANKS = (3, 6, 7)
    YB = (E + 1) * TT // 2
    EARLY, LATE = range(TT // 2), range(TT // 2, TT)
    LN_STEPS = 2
    GATE_STAGES = 10

    with nc.Block() as block:
        def over_chunks(body, apart=1):
            def run(eng):
                with eng.Fori(0, NCH // 2 - apart) as i:
                    for u in range(2):
                        body(eng, i, u, 2 * i + u, 2 * apart)
                for n in range(NCH - 2 * apart, NCH):
                    body(eng, n // 2, n % 2, n, NCH - 1 - n)
            return run

        @block.sync
        def _(sp):
            sp.wait_ge(att_ready, 1)
            sp.wait_ge(x_added, 1)
            chunks.load(sp, 2, 0)

            def body(sp, i, u, n, ahead):
                if ahead >= 3:
                    sp.wait_ge(att_ready, n + 2)
                    wait_alone(sp, x_added, n + 2, passed)
                    chunks.load(sp, n + 3, 1 - u)
                wait_alone(sp, y_added, done(n) * YB, passed)
                sp.dma_start(out[bass.ds(n * CH, CH), :].rearrange("(t p) d -> p t d", p=P), y[u][:])\
                  .then_inc(out_stored[u], 16)

            over_chunks(body, apart=2)(sp)
            for u in range(2):
                sp.wait_ge(out_stored[u], 16 * (NCH // 2 + 1))

        @block.tensor
        def _(pe):
            def projected(n, u, tiles):
                pe.wait_ge(att_ready, n + 1)
                for t in tiles:
                    for k in range(KD):
                        for i, (a, z) in enumerate(PRODUCTS):
                            mm = pe.matmul(bank[:, 4 + t // 2, (t % 2) * D:(t % 2 + 1) * D],
                                           att[u][a][:, k, t * P:(t + 1) * P], wo_sb[z][:, k, :],
                                           start=(k + i == 0), stop=(k == KD - 1 and i == 2))
                mm.then_inc(o_summed, 1)

            def turned(n, u):
                pe.wait_ge(xn_ready, done(n))
                pe.wait_ge(xnT_ready, done(n) - 1)
                for k in range(KD):
                    for t in range(TT):
                        mm = pe.transpose(bank[:, 4 + k, t * P:(t + 1) * P], xn[u][:, t, k * P:(k + 1) * P], ident_sb[:])
                mm.then_inc(xnT_summed, 1)

            def routed(n, u):
                pe.wait_ge(xnT_ready, done(n))
                for k in range(KD):
                    for t in range(TT):
                        mm = pe.matmul(bank[32 * t:32 * (t + 1), 2, 0:P], route[:, k, :],
                                       xnT32[u][:, k, t * P:(t + 1) * P], start=(k == 0), stop=(k == KD - 1))
                mm.then_inc(scoresT_summed, 1)

            def scored_back(n):
                pe.wait_ge(scoresT_ready, n + 1)
                pe.transpose(bank[:, 2, P:2 * P], scoresT[:], ident_sb[:]).then_inc(scores_summed, 1)

            def first_product(n, u, e):
                pe.wait_ge(xnT_ready, done(n))
                pe.wait_ge(hid32_ready, n * E + e - 1 + LEAD * E)
                for k in range(KD):
                    for i, (a, z) in enumerate(PRODUCTS):
                        mm = pe.matmul(bank[:, e % 2, :], w1_sb[a][:, k, e, :], xnT[u][z][:, k, :],
                                       start=(k + i == 0), stop=(k == KD - 1 and i == 2))
                mm.then_inc(hid_summed, 1)

            def second_product(n, e):
                pe.wait_ge(hid_ready, n * E + e + 1)
                for t in range(TT):
                    m = e * TT // 2 + t // 2
                    if t % 2 == 0:
                        pe.wait_ge(y_added, n * YB + m - 2 + LEAD * YB)
                    for i, (a, z) in enumerate(PRODUCTS):
                        mm = pe.matmul(bank[:, Y_BANKS[m % 3], (t % 2) * D:(t % 2 + 1) * D],
                                       hid[a][:, e, t * P:(t + 1) * P], w2_sb[z][:, e, :],
                                       start=(i == 0), stop=(i == 2))
                    if t % 2 == 1:
                        mm.then_inc(y_summed, 1)

            def turned_gates(n):
                pe.wait_ge(gate_halves_ready, n + 1)
                for t in range(TT):
                    mm = pe.transpose(bank[0:3 * E, 2, t * P:(t + 1) * P], gate_halves[:, t, :].bitcast(F32), ident_sb[:])
                mm.then_inc(gatesT_summed, 1)

            def last_bias(n):
                pe.wait_ge(gatesT_ready, n + 1)
                for t in range(TT):
                    m = E * TT // 2 + t // 2
                    if t % 2 == 0:
                        pe.wait_ge(y_added, n * YB + m - 2 + LEAD * YB)
                    mm = pe.matmul(bank[:, Y_BANKS[m % 3], (t % 2) * D:(t % 2 + 1) * D],
                                   gatesT[:, t * P:(t + 1) * P], b2_sb[:], start=True, stop=True)
                    if t % 2 == 1:
                        mm.then_inc(y_summed, 1)

            pe.sem_inc(xnT_summed, LEAD)
            for k in range(KD):
                pe.transpose(bank[:, 2, k * 2 * E:k * 2 * E + E], cent_sb[:, k * P:(k + 1) * P], ident_sb[0:E, 0:E])
                mm = pe.transpose(bank[:, 2, k * 2 * E + E:(k + 1) * 2 * E], wr_sb[:, k * P:(k + 1) * P], ident_sb[0:E, 0:E])
            mm.then_inc(routeT_summed, 1)
            for tiles in (EARLY, LATE):
                projected(0, 0, tiles)
            pe.wait_ge(route_ready, 2)
            turned(0, 0)
            for e in range(E):
                first_product(0, 0, e)
                if e == 1:
                    for tiles in (EARLY, LATE):
                        projected(1, 1, tiles)
            turned(1, 1)
            routed(0, 0)
            scored_back(0)

            def body(pe, i, u, n, ahead):
                for e in range(E):
                    second_product(n, e)
                    if e == E - 1 and ahead >= 2:
                        turned(n + 2, u)
                    if ahead >= 1:
                        first_product(n + 1, 1 - u, e)
                    if e == 0:
                        turned_gates(n)
                    if e == 1 and ahead >= 1:
                        pe.wait_ge(gatesT_ready, n + 1)
                        routed(n + 1, 1 - u)
                    if e == 2 and ahead >= 1:
                        scored_back(n + 1)
                    if e in (2, 3) and ahead >= 2:
                        projected(n + 2, u, (EARLY, LATE)[e - 2])
                last_bias(n)

            over_chunks(body)(pe)

        @block.scalar
        def _(act):
            act.sem_inc(hid32_ready, LEAD * E)

            def att_highs(n, i, u):
                act.wait_ge(att_loaded[u], 32 * (i + 1))
                act.wait_ge(o_summed, 2 * (n - 1)) if not isinstance(n, int) or n >= 2 else None
                nc.scalar.copy(att[u][0][:], att_sb[u][:]).then_inc(att_high, 1)

            def turned(n, u):
                act.wait_ge(xnT_summed, done(n))
                nc.scalar.copy(xnT[u][0][:], bank[:, 4:4 + KD, :]).then_inc(xnT_high_ready, 1)
                nc.scalar.copy(xnT32[u][:], bank[:, 4:4 + KD, :]).then_inc(xnT_high_ready, 1)

            def scores_out(n):
                act.wait_ge(scoresT_summed, n + 1)
                nc.scalar.copy(scoresT[:], bank[:, 2, 0:P]).then_inc(scoresT_ready, 1)

            def exped(n):
                act.wait_ge(gate_step, n * GATE_STAGES + 6)
                nc.scalar.activation(exps[:], shifted[:], ACT.Exp).then_inc(exps_ready, 1)

            def hidden(n, e):
                act.wait_ge(hid_summed, n * E + e + 1)
                if not isinstance(n, int) or n * E + e >= HB:
                    act.wait_ge(hid_ready, n * E + e + 1 - HB)
                nc.scalar.activation(hid32[e % HB][:], bank[:, e % 2, :], ACT.Gelu, bias=b1_sb[:, e:e + 1])\
                  .then_inc(hid32_ready, 1)
                act.wait_ge(hid32_ready, n * E + e + 1 + LEAD * E)
                nc.scalar.copy(hid[0][:, e, :], hid32[e % HB][:]).then_inc(hid_high, 1)

            att_highs(0, 0, 0)
            att_highs(1, 0, 1)
            turned(0, 0)
            for e in range(E):
                hidden(0, e)
            turned(1, 1)
            scores_out(0)
            exped(0)

            def body(act, i, u, n, ahead):
                for e in range(E):
                    if e == E - 1 and ahead >= 2:
                        turned(n + 2, u)
                    if ahead >= 1:
                        hidden(n + 1, e)
                    if e == 0:
                        act.wait_ge(gatesT_summed, n + 1)
                        nc.scalar.copy(gatesT[:], bank[0:3 * E, 2, :]).then_inc(gatesT_ready, 1)
                        if ahead >= 2:
                            att_highs(n + 2, i + 1, u)
                    if e == 1 and ahead >= 1:
                        scores_out(n + 1)
                    if e == 5 and ahead >= 1:
                        exped(n + 1)

            over_chunks(body)(act)

        @block.gpsimd
        def _(pool):
            nc.gpsimd.memset(minus_half[:], -0.5).then_inc(consts_set, 1)
            nc.gpsimd.memset(half[:], 0.5).then_inc(consts_set, 1)
            pool.wait_ge(consts_set, 2)

            def roots(n):
                pool.wait_ge(var_ready, n + 1)
                nc.gpsimd.tensor_tensor(rstd[:], var_eps[:], minus_half[:], ALU.pow).then_inc(rstd_ready, 1)
                nc.gpsimd.tensor_tensor(root[:], sq[:], half[:], ALU.pow).then_inc(rstd_ready, 1)

            def att_lows(n, u):
                pool.wait_ge(att_high, n + 1)
                nc.gpsimd.tensor_tensor(att[u][1][:], att_sb[u][:], att[u][0][:].bitcast(F32),
                                        ALU.subtract).then_inc(att_ready, 1)

            def x_and_bias(n, i, u):
                pool.wait_ge(att_loaded[u], 32 * (i + 1))
                if not isinstance(n, int) or n >= 2:
                    pool.wait_ge(y_added, (n - 2) * YB + 2 + LEAD * YB)
                nc.gpsimd.tensor_tensor(x2[u][:], x_sb[u][:], bo_sb[:], ALU.add).then_inc(x_added, 1)

            def low(n, e):
                pool.wait_ge(hid_high, n * E + e + 1)
                nc.gpsimd.tensor_tensor(hid[1][:, e, :], hid32[e % HB][:], hid[0][:, e, :].bitcast(F32),
                                        ALU.subtract).then_inc(hid_ready, 1)

            att_lows(0, 0)
            x_and_bias(0, 0, 0)
            att_lows(1, 1)
            roots(0)
            x_and_bias(1, 0, 1)
            for e in range(E):
                low(0, e)
                if e == 1:
                    roots(1)

            def body(pool, i, u, n, ahead):
                for e in range(E):
                    if e == 5 and ahead >= 2:
                        roots(n + 2)
                    if ahead >= 1:
                        low(n + 1, e)
                    if e == 0 and ahead >= 2:
                        att_lows(n + 2, u)
                    if e == 2 and ahead >= 2:
                        x_and_bias(n + 2, i + 1, u)

            over_chunks(body)(pool)

        @block.vector
        def _(dve):
            dve.sem_inc(xn_ready, LEAD)
            dve.sem_inc(xnT_ready, LEAD)
            nc.vector.memset(route[:], 0.0).then_inc(route_ready, 1)
            dve.sem_inc(y_added, LEAD * YB)
            for u in range(2):
                dve.sem_inc(out_stored[u], 16)
            dve.wait_ge(routeT_summed, 1)
            dve.wait_ge(route_ready, 1)
            nc.vector.tensor_copy(route[:, :, 0:2 * E], bank[:, 2, 0:KD * 2 * E].rearrange("p (k e) -> p k e", k=KD))\
              .then_inc(route_ready, 1)

            def lows(n, u):
                dve.wait_ge(xnT_high_ready, 2 * (n + 1))
                nc.vector.tensor_tensor(xnT[u][1][:], bank[:, 4:4 + KD, :], xnT[u][0][:].bitcast(F32),
                                        ALU.subtract).then_inc(xnT_ready, 1)

            def norm(n, u, stage):
                if stage == 0:
                    dve.wait_ge(x_added, n + 1)
                    dve.wait_ge(o_summed, 2 * (n + 1))
                    nc.vector.tensor_tensor(x2[u][:], bank[:, 4:6, :].rearrange("p a (b d) -> p (a b) d", b=2), x2[u][:],
                                            ALU.add).then_inc(x2_ready, 1)
                if stage in (1, 2):
                    dve.wait_ge(x2_ready, n + 1)
                    for t in (EARLY, LATE)[stage - 1]:
                        ins = nc.vector.bn_stats(stats[:, t], x2[u][:, t])
                    if stage == 2:
                        ins.then_inc(ln_step, 1)
                if stage == 3:
                    wait_alone(dve, ln_step, n * LN_STEPS + 1, passed)
                    for t in range(TT):
                        ins = nc.vector.bn_aggr(mv[:, t], stats[:, t])
                    ins.then_inc(ln_step, 1)
                    dve.wait_ge(ln_step, n * LN_STEPS + 2)
                    nc.vector.tensor_scalar(sq[:], mv[:, :, 1], float(D), None, ALU.mult)
                    nc.vector.tensor_scalar(var_eps[:], mv[:, :, 1], 1e-5, None, ALU.add).then_inc(var_ready, 1)
                if stage == 4:
                    dve.wait_ge(rstd_ready, 2 * n + 1)
                    dve.wait_ge(xnT_summed, two_before(n))
                if stage in (4, 5):
                    for t in (EARLY, LATE)[stage - 4]:
                        ins = nc.vector.tensor_scalar(xn[u][:, t], x2[u][:, t], mv[:, t, 0:1], rstd[:, t:t + 1],
                                                      ALU.subtract, ALU.mult)
                if stage == 5:
                    ins.then_inc(xn_ready, 1)
                    dve.wait_ge(rstd_ready, 2 * (n + 1))
                    nc.vector.tensor_tensor(length[u][:], root[:], rstd[:], ALU.mult).then_inc(length_ready, 1)

            def gate(n, u, stage):
                def link(ins):
                    ins.then_inc(gate_step, 1)

                if stage > GATE_STAGES:
                    pass
                elif stage == 4:
                    wait_alone(dve, gate_step, n * GATE_STAGES + stage, passed)
                elif stage > 0:
                    dve.wait_ge(gate_step, n * GATE_STAGES + stage)
                if stage == 0:
                    dve.wait_ge(length_ready, n + 1)
                    link(nc.vector.tensor_scalar(length[u][:], length[u][:], 1e-12, None, ALU.max))
                if stage == 1:
                    link(nc.vector.reciprocal(length[u][:], length[u][:]))
                if stage == 2:
                    dve.wait_ge(scores_summed, n + 1)
                    link(nc.vector.tensor_copy(scored[:], bank[:, 2, P:2 * P].rearrange("p (t e) -> p t e", t=TT)[:, :, 0:2 * E]))
                if stage == 3:
                    for t in range(TT):
                        ins = nc.vector.scalar_tensor_tensor(out=logits[:, t], in0=scored[:, t, 0:E],
                                                             scalar=length[u][:, t:t + 1],
                                                             in1=scored[:, t, E:2 * E], op0=ALU.mult, op1=ALU.add)
                    link(ins)
                if stage == 4:
                    for t in range(TT):
                        ins = nc.vector.max(top[:, t], logits[:, t])
                    link(ins)
                if stage == 5:
                    link(nc.vector.tensor_tensor(shifted[:], logits[:], top[:, :, 0:1].to_broadcast([P, TT, E]),
                                                 ALU.subtract))
                if stage == 6:
                    link(nc.vector.tensor_tensor(kept[:], logits[:], top[:, :, 1:2].to_broadcast([P, TT, E]), ALU.is_ge))
                if stage == 7:
                    dve.wait_ge(exps_ready, n + 1)
                    link(nc.vector.tensor_tensor(kept[:], kept[:], exps[:], ALU.mult))
                if stage == 8:
                    link(nc.vector.tensor_reduce(total[:], kept[:], AX.X, ALU.add))
                if stage == 9:
                    link(nc.vector.reciprocal(total[:], total[:]))
                if stage == 10:
                    nc.vector.tensor_tensor(gates[u][:], kept[:], total[:].unsqueeze(2).to_broadcast([P, TT, E]),
                                            ALU.mult).then_inc(gates_ready, 1)
                if stage == 11:
                    dve.wait_ge(gates_ready, n + 1)
                    if not isinstance(n, int) or n >= 1:
                        dve.wait_ge(gatesT_summed, n)
                    both = gate_halves[:].rearrange("p t (r e) -> p t r e", r=3)[:, :, 0:3:2, :]
                    nc.vector.tensor_copy(both, gates[u][:].unsqueeze(2).to_broadcast([P, TT, 2, E])).then_inc(gates_high, 1)
                if stage == 12:
                    dve.wait_ge(gates_high, n + 1)
                    nc.vector.tensor_tensor(gate_halves[:, :, E:2 * E], gates[u][:], gate_halves[:, :, 0:E].bitcast(F32),
                                            ALU.subtract).then_inc(gate_halves_ready, 1)

            def add(n, i, u, m):
                e, a = m // 2, m % 2
                dve.wait_ge(y_summed, n * YB + m + 1)
                if m >= 2:
                    dve.wait_ge(y_added, n * YB + m - 1 + LEAD * YB)
                if e < E:
                    for t in (2 * a, 2 * a + 1):
                        ins = nc.vector.scalar_tensor_tensor(
                            out=acc[u][:, t], in0=bank[:, Y_BANKS[m % 3], (t % 2) * D:(t % 2 + 1) * D],
                            scalar=gates[u][:, t, e:e + 1], in1=(x2 if e == 0 else acc)[u][:, t],
                            op0=ALU.mult, op1=ALU.add)
                else:
                    if a == 0:
                        dve.wait_ge(out_stored[u], 16 * (i + 1))
                    ins = nc.vector.tensor_tensor(y[u][:, 2 * a:2 * a + 2],
                                                  bank[:, Y_BANKS[m % 3], :].rearrange("p (b d) -> p b d", b=2),
                                                  acc[u][:, 2 * a:2 * a + 2], ALU.add)
                ins.then_inc(y_added, 1)

            for stage in range(6):
                norm(0, 0, stage)
            lows(0, 0)
            for stage in range(6):
                norm(1, 1, stage)
            lows(1, 1)
            for stage in range(GATE_STAGES + 3):
                gate(0, 0, stage)

            gate_at = (4, 5, 6, 7, 8, 9, 10, 12, 13, 14, 15, 16, 17)
            norm_at = (7, 8, 9, 10, 11, 12)

            def body(dve, i, u, n, ahead):
                dve.wait_ge(gates_ready, n + 1)
                for m in range(YB):
                    add(n, i, u, m)
                    if ahead >= 1 and m in gate_at:
                        gate(n + 1, 1 - u, gate_at.index(m))
                    if ahead >= 2 and m in norm_at:
                        norm(n + 2, u, norm_at.index(m))
                    if ahead >= 2 and m == 16:
                        lows(n + 2, u)

            over_chunks(body)(dve)


def kernel(**inputs):
    import numpy as np
    import concourse.bacc as bacc
    from concourse.bass_utils import run_bass_kernel_spmd

    def f(name):
        return np.asarray(inputs[name])

    inv_freq = (np.float32(1.0) / np.power(np.float32(10000.0), np.arange(0, HD, 2, dtype=np.float32) / np.float32(HD)))
    angle = np.arange(N, dtype=np.float32)[:, None] * inv_freq.astype(np.float32)[None, :]
    row = np.arange(P) % HD // 2
    cos = np.cos(angle).astype(np.float32).T[row]
    sin = np.sin(angle).astype(np.float32).T[row] * np.where(np.arange(P) % 2 == 0, -1, 1).astype(np.float32)[:, None]
    tri = (np.arange(P)[None, :] >= np.arange(P)[:, None]).astype(np.float32)
    causal = np.where(np.arange(2 * N - P)[None, :] - (N - P) <= np.arange(P)[:, None], 0.0, -10000.0).astype(np.float32)
    arrays = {
        "x": f("L0_attn_x").reshape(B * N, D),
        "wqkv": np.concatenate([f("L0_attn_Wq").T, f("L0_attn_Wk").T, f("L0_attn_Wv").T], axis=1),
        "wo": f("L0_attn_Wo").T, "bo": f("L0_attn_bo").reshape(1, D),
        "w1": f("L0_ffn_w1"), "b1": f("L0_ffn_b1").T, "w2": f("L0_ffn_w2"), "b2": f("L0_ffn_b2"),
        "lowest": np.repeat(np.array([[0.0], [0.0], [-1.0]], dtype=np.float32), E, axis=0),
        "cent": f("L0_ffn_centroids"), "wr": f("L0_ffn_w_route"),
        "causal": causal, "head_mask": np.kron(np.eye(P // HD), np.ones((HD, HD))).astype(np.float32),
        "cos": cos, "sin": sin, "tri": np.stack([tri, tri], axis=1), "ident": np.eye(P, dtype=np.float32),
    }
    arrays = {k: np.ascontiguousarray(a) for k, a in arrays.items()}
    nc = bacc.Bacc("TRN2", target_bir_lowering=False, num_devices=1)
    aps = {k: nc.dram_tensor(k, a.shape, mybir.dt.from_np(a.dtype), kind="ExternalInput").ap() for k, a in arrays.items()}
    out = nc.dram_tensor("out", (B * N, D), F32, kind="ExternalOutput").ap()
    layer_kernel(nc, **aps, out=out)
    r = run_bass_kernel_spmd(nc, [arrays], core_ids=[0])
    return r.results[0]["out"].reshape(B, N, D)
```
